# Optimizing a Trainium2 kernel written in Bass

```python
import numpy as np
import jax
import jax.numpy as jnp

def _softmax(x, axis=-1):
    return jax.nn.softmax(x, axis=axis)

def _gelu(x):
    return jax.nn.gelu(x, approximate=True)

def _silu(x):
    return jax.nn.silu(x)

def _sigmoid(x):
    return jax.nn.sigmoid(x)

def _layernorm(x, axis=-1, eps=1e-05):
    m = jnp.mean(x, axis=axis, keepdims=True)
    v = jnp.var(x, axis=axis, keepdims=True)
    return (x - m) / jnp.sqrt(v + eps)

def _scatter_add(tgt, idx, src, axis=0):
    return tgt.at[idx].add(src)

def _segment_sum(src, seg, n):
    return jax.ops.segment_sum(src, seg, n)
kernel_name = 'mk_seq_preln_d1_jaxref_r8_85ff47'

def setup_inputs(seed: int=0):
    np.random.seed(seed)
    _w = jnp.asarray

    def _L0_attn_setup():
        import jax, jax.numpy as jnp
        import numpy as np
        N_EMBD = 128
        N_HEAD = 16
        HEAD_DIM = N_EMBD // N_HEAD
        LATENT_DIM = N_EMBD // 2
        B, T = (4, 256)
        key = jax.random.key(seed)
        ks = jax.random.split(key, 5)

        def init(k, fan_in, fan_out):
            bound = 1.0 / np.sqrt(fan_in)
            return jax.random.uniform(k, (fan_in, fan_out), jnp.float32, -bound, bound)
        return {'x': jax.random.normal(ks[0], (B, T, N_EMBD), jnp.float32), 'Wc_down': init(ks[1], N_EMBD, LATENT_DIM), 'Wq_up': init(ks[2], LATENT_DIM, N_EMBD), 'Wkv_up': init(ks[3], LATENT_DIM, 2 * HEAD_DIM), 'Wc_proj': init(ks[4], N_EMBD, N_EMBD)}
    _L0_attn_in = _L0_attn_setup()

    def _L0_ffn_setup():
        import jax, jax.numpy as jnp
        import numpy as np
        B, S, D_IN, D_OUT = (16, 512, 128, 128)
        ACT_BITS = 8
        QB = float(2 ** (ACT_BITS - 1) - 1)
        key = jax.random.key(seed)
        k1, k2, k3 = jax.random.split(key, 3)
        x = jax.random.normal(k1, (B, S, D_IN), dtype=jnp.float32)
        ternary_weight = jax.random.randint(k2, (D_OUT, D_IN), 0, 3, dtype=jnp.int32)
        bias = jax.random.normal(k3, (D_OUT,), dtype=jnp.float32)
        act_scale = (jnp.max(jnp.abs(x)) / QB).astype(jnp.float32)
        return {'x': x, 'ternary_weight': ternary_weight, 'bias': bias, 'act_scale': act_scale}
    _L0_ffn_in = _L0_ffn_setup()
    _d = {'L0_attn_x': _L0_attn_in['x'], 'L0_attn_Wc_down': _L0_attn_in['Wc_down'], 'L0_attn_Wq_up': _L0_attn_in['Wq_up'], 'L0_attn_Wkv_up': _L0_attn_in['Wkv_up'], 'L0_attn_Wc_proj': _L0_attn_in['Wc_proj'], 'L0_ffn_ternary_weight': _L0_ffn_in['ternary_weight'], 'L0_ffn_bias': _L0_ffn_in['bias'], 'L0_ffn_act_scale': _L0_ffn_in['act_scale']}
    _x0 = _d['L0_attn_x']
    _d['L0_attn_x'] = jax.random.normal(jax.random.fold_in(jax.random.key(seed), 1), (16, 512, 128), dtype=_x0.dtype)
    del _x0
    return _d

def reference(L0_attn_x, L0_attn_Wc_down, L0_attn_Wq_up, L0_attn_Wkv_up, L0_attn_Wc_proj, L0_ffn_ternary_weight, L0_ffn_bias, L0_ffn_act_scale):

    def _L0_attn_ref(x, Wc_down, Wq_up, Wkv_up, Wc_proj):
        import jax, jax.numpy as jnp
        import numpy as np
        N_EMBD = 128
        N_HEAD = 16
        HEAD_DIM = N_EMBD // N_HEAD
        LATENT_DIM = N_EMBD // 2
        B, T = (4, 256)
        Bsz, Tlen, C = x.shape
        latent = x @ Wc_down
        q = (latent @ Wq_up).reshape(Bsz, Tlen, N_HEAD, HEAD_DIM)
        kv = latent @ Wkv_up
        k, v = (kv[..., :HEAD_DIM], kv[..., HEAD_DIM:])
        scale = 1.0 / np.sqrt(HEAD_DIM)
        att = jnp.einsum('bthd,bsd->bhts', q, k) * scale
        causal = jnp.tril(jnp.ones((Tlen, Tlen), dtype=bool))
        att = jnp.where(causal[None, None], att, -jnp.inf)
        att = jax.nn.softmax(att, axis=-1)
        y = jnp.einsum('bhts,bsd->bthd', att, v).reshape(Bsz, Tlen, C)
        return y @ Wc_proj

    def _L0_ffn_ref(x, ternary_weight, bias, act_scale):
        import jax, jax.numpy as jnp
        import numpy as np
        B, S, D_IN, D_OUT = (16, 512, 128, 128)
        ACT_BITS = 8
        QB = float(2 ** (ACT_BITS - 1) - 1)
        scale = jnp.maximum(act_scale, 1e-05)
        x_int = jnp.clip(jnp.round(x / scale), -QB, QB)
        x_dq = jnp.nan_to_num(x_int * scale, nan=0.0, posinf=10000.0, neginf=-10000.0)
        w = ternary_weight.astype(jnp.float32) - 1.0
        return jnp.einsum('bsi,oi->bso', x_dq, w) + bias
    x = L0_attn_x
    x = x + _L0_attn_ref(_layernorm(x, axis=-1), L0_attn_Wc_down, L0_attn_Wq_up, L0_attn_Wkv_up, L0_attn_Wc_proj)
    x = x + _L0_ffn_ref(_layernorm(x, axis=-1), L0_ffn_ternary_weight, L0_ffn_bias, L0_ffn_act_scale)
    return x

_drawn_inputs = setup_inputs


def setup_inputs(seed=0):
    import zlib

    import numpy as np

    out = dict(_drawn_inputs(seed))
    spreads = {}
    factors = {'L0_attn_Wq_up': 6.241}
    for name, (base, spread) in spreads.items():
        noise = np.random.default_rng([zlib.crc32(name.encode()), seed]).standard_normal(out[name].shape)
        drawn = base * np.exp(spread * noise) if base else spread * noise
        out[name] = jnp.asarray(drawn.astype(out[name].dtype))
    for name, factor in factors.items():
        out[name] = (out[name] * factor).astype(out[name].dtype)
    return out
```

```python
from contextlib import ExitStack

import concourse.bass as bass
from concourse import mybir

F32 = mybir.dt.float32
BF16 = mybir.dt.bfloat16
I32 = mybir.dt.int32
ALU = mybir.AluOpType
ACT = mybir.ActivationFunctionType
AX_X = mybir.AxisListType.X

NB, T, C = 16, 512, 128
H, D = 16, 8
LATENT = 64
NT = T // 128
PARTS = 3
KQ = PARTS * PARTS * D
GRP = 16
R_MASK = KQ
K_MAX = 96
R_M = 96
K_S = R_M + PARTS
TQ = 8
NTILE = T // TQ
NEG = -1.0e38
SCALE = 1.0 / float(D) ** 0.5
EPS = 1e-5
QB = 127.0
ROUND = 12582912.0
BIGGEST = 3.0e38
RING = 3

HQ = 4
MASKS = 28
CHUNKS = 20
UNITS = 12
SLOTS = UNITS
STEPS = [(g, (2 * g, 2 * g + 1)) for g in range(16)] + [(i // 2, (i,)) for i in range(32, NTILE)]
NSTEP = len(STEPS)


def step_places():
    cost = [len(tiles) * GRP * (g + 1) + 100 for g, tiles in STEPS]
    total, at, out = sum(cost), 0, [[] for _ in range(4 * SLOTS)]
    for k, c in enumerate(cost):
        out[min(4 * SLOTS - 1, int((at + c / 2) * 4 * SLOTS / total))].append(k)
        at += c
    return out


PLACES = step_places()

def has_q(it): return 0 <= it < NB
def has_m(it): return 0 <= it - 1 < NB
def has_b(it): return 0 <= it - 2 < NB
def has_c(it): return 0 <= it - 3 < NB

LAST_TURN = NB + 3
STEADY = (3, NB - 1)
AUX = [("Qtr", has_q), ("Qq", has_q), ("Cproj", has_c), ("Qk", has_q), ("Qv", has_q),
       ("Ctr", has_c), ("Cffn", has_c), ("Msel", has_m)]


def aux_use(it, name):
    if isinstance(it, int):
        before = sum(on(e) for e in range(it) for _, on in AUX)
        for n, on in AUX:
            if n == name:
                return before
            before += on(it)
    start = sum(on(e) for e in range(STEADY[0]) for _, on in AUX)
    return (it - STEADY[0]) * len(AUX) + (start + [n for n, _ in AUX].index(name))


def wait(eng, sem, value):
    if not isinstance(value, int) or value > 0:
        eng.wait_ge(sem, value)


def program(nc, x, w_down, w_q, w_kv, w_proj, w_tern, bias, act_scale, out):
    with ExitStack() as ctx:
        def sb(name, shape, dt):
            return ctx.enter_context(nc.sbuf_tensor(name, shape, dt))

        def sem(name):
            return ctx.enter_context(nc.semaphore(name))

        score_ps = ctx.enter_context(nc.psum_tensor("score_ps", [128, 4, 512], F32))
        pv_ps = ctx.enter_context(nc.psum_tensor("pv_ps", [128, 512], F32))
        max_ps = ctx.enter_context(nc.psum_tensor("max_ps", [128, 2, 512], F32))
        aux_ps = ctx.enter_context(nc.psum_tensor("aux_ps", [128, 512], F32))

        ident = sb("ident", [128, 128], F32)
        ident_b = sb("ident_b", [128, 128], BF16)
        select = sb("select", [128, TQ, 32], BF16)
        half_neg = sb("half_neg", [128, NT], F32)
        part_row = sb("part_row", [1, 2, PARTS, PARTS, D], F32)
        part_col = sb("part_col", [KQ, 2], F32)
        wd_sb = sb("wd_sb", [128, LATENT], F32)
        wdT_sb = sb("wdT_sb", [LATENT, 128], F32)
        wq_sb = sb("wq_sb", [LATENT, C], F32)
        wkv_sb = sb("wkv_sb", [LATENT, 2 * D], F32)
        wdq = sb("wdq", [128, C], F32)
        wdk = sb("wdk", [128, PARTS * PARTS, D], F32)
        wdv = sb("wdv", [128, D], F32)
        wp_sb = sb("wp_sb", [128, C], F32)
        wt_i = sb("wt_i", [128, C], I32)
        wt_b = sb("wt_b", [128, C], BF16)
        wt_T = sb("wt_T", [128, C], BF16)
        bias_sb = sb("bias_sb", [128, C], F32)
        scale_sb = sb("scale_sb", [128, 4], F32)

        xa = sb("xa", [128, RING, NT, C], F32)
        st1 = sb("st1", [128, NT, 6], F32)
        mv1 = sb("mv1", [128, NT, 2], F32)
        ln1 = sb("ln1", [128, 4, NT], F32)
        xn = sb("xn", [128, NT, C], F32)
        xnT = sb("xnT", [128, T], F32)
        q1 = sb("q1", [128, T], BF16)
        q_r = sb("q_r", [128, T], F32)
        q2 = sb("q2", [128, T], BF16)
        q3 = sb("q3", [128, T], BF16)
        k1 = sb("k1", [KQ, T], BF16)
        k_r = sb("k_r", [KQ, T], F32)
        k2 = sb("k2", [KQ, T], BF16)
        kf = sb("kf", [KQ, T], BF16)
        q_rows = [sb(f"q_rows{n}", [128, H, TQ, NTILE], BF16) for n in range(RING)]
        k_rows = [sb(f"k_rows{n}", [128, T], BF16) for n in range(RING)]
        k_mask = [sb(f"k_mask{n}", [128, T], BF16) for n in range(RING)]
        v_ones = [sb(f"v_ones{n}", [128, NT, 32], F32) for n in range(RING)]
        neg_max = sb("neg_max", [128, NTILE], F32)
        m_r = sb("m_r", [128, 2, NTILE], F32)
        m_parts = sb("m_parts", [128, PARTS, NTILE], BF16)
        m_rows = sb("m_rows", [32 * PARTS, T], BF16)
        probs = [sb(f"probs{n}", [128, w], F32) for n, w in enumerate((2048, 2048, 1024))]
        y_raw = sb("y_raw", [128, 2, T], F32)
        y_num = sb("y_num", [128, T], F32)
        y_den = sb("y_den", [128, T], F32)
        y_inv = sb("y_inv", [128, T], F32)
        yT = sb("yT", [128, T], F32)
        xr = sb("xr", [128, NT, C], F32)
        x1 = sb("x1", [128, NT, C], F32)
        x1b = sb("x1b", [128, NT, C], F32)
        st2 = sb("st2", [128, NT, 6], F32)
        mv2 = sb("mv2", [128, NT, 2], F32)
        ln2 = sb("ln2", [128, 5, NT], F32)
        z = sb("z", [128, NT, C], F32)
        z_neg = sb("z_neg", [128, NT, C], F32)
        z_lo = sb("z_lo", [128, NT, C], F32)
        xq = sb("xq", [128, NT, C], BF16)
        xqT = sb("xqT", [128, T], BF16)
        o_sb = sb("o_sb", [128, NT, C], F32)

        w_loaded = sem("w_loaded")
        pool_set = sem("pool_set")
        dve_set = sem("dve_set")
        act_set = sem("act_set")
        pe_set = sem("pe_set")
        part_moved = sem("part_moved")
        x_loaded = sem("x_loaded")
        ln1_stats = sem("ln1_stats")
        ln1_aggr = sem("ln1_aggr")
        ln1_step = sem("ln1_step")
        xn_done = sem("xn_done")
        aux_filled = sem("aux_filled")
        aux_free = sem("aux_free")
        q1_done = sem("q1_done")
        q2_done = sem("q2_done")
        q3_done = sem("q3_done")
        k1_done = sem("k1_done")
        k2_done = sem("k2_done")
        kf_done = sem("kf_done")
        q_moved = sem("q_moved")
        k_moved = sem("k_moved")
        max_ready = sem("max_ready")
        max_done = sem("max_done")
        m_split = sem("m_split")
        m_moved = sem("m_moved")
        score_ready = sem("score_ready")
        exp_done = sem("exp_done")
        masked = sem("masked")
        pv_done = sem("pv_done")
        pv_copied = sem("pv_copied")
        y_moved = [sem(f"y_moved{n}") for n in range(2)]
        inv_done = sem("inv_done")
        y_ready = sem("y_ready")
        xr_loaded = sem("xr_loaded")
        ln2_stats = sem("ln2_stats")
        ln2_aggr = sem("ln2_aggr")
        ln2_step = sem("ln2_step")
        z_step = sem("z_step")
        xq_done = sem("xq_done")
        x1b_done = sem("x1b_done")
        o_stored = sem("o_stored")

        carried = sem("carried")

        N_WEIGHTS = 6 + HQ * 4
        POOL_SET = 10 + 7 * RING
        Y_MOVES = 16 * 2 * 4

        def tokens(dram):
            return dram.rearrange("(n p) c -> p n c", p=128)

        def halves(dram):
            v = dram.rearrange("(i n a) c -> a i n c", n=NT, a=2)
            return v[0], v[1]

        def apart(eng, value):
            if not isinstance(value, int):
                eng.sem_inc(carried, 1)

        def positions(a):
            return a[:, :].rearrange("p (a i) -> p a i", a=TQ)

        def by_position(a):
            return a[:, :].rearrange("p (i a) -> p a i", a=TQ)

        def run_turns(eng, turn):
            for it in range(STEADY[0]):
                turn(it, it % RING)
            with eng.Fori(0, (STEADY[1] - STEADY[0]) // RING) as i:
                for u in range(RING):
                    turn(i * RING + (STEADY[0] + u), (STEADY[0] + u) % RING)
            for it in range(STEADY[1], LAST_TURN):
                turn(it, it % RING)

        def on(it, stage):
            return stage(it) if isinstance(it, int) else True

        block = ctx.enter_context(nc.Block())

        @block.sync
        def _(sp):
            sp.dma_start(xa[:, 0], tokens(x[0])).then_inc(x_loaded, 16)
            sp.dma_start(wd_sb[:, :], w_down).then_inc(w_loaded, 16)
            sp.dma_start(wq_sb[:, :], w_q).then_inc(w_loaded, 16)
            sp.dma_start(wkv_sb[:, :], w_kv).then_inc(w_loaded, 16)
            sp.dma_start(wt_i[:, :], w_tern).then_inc(w_loaded, 16)
            sp.dma_start(bias_sb[:, :], bias.rearrange("(a c) -> a c", a=1).broadcast_to([128, C])).then_inc(w_loaded, 16)
            sp.dma_start(scale_sb[:, 0:1], act_scale.broadcast_to([128, 1])).then_inc(w_loaded, 16)
            for r in range(4):
                for hq in range(HQ):
                    head, row = 4 * hq + r, 32 * r + D * hq
                    sp.dma_start(wp_sb[row:row + D, :], w_proj[D * head:D * head + D, :]).then_inc(w_loaded, 16)
            sp.wait_ge(pool_set, POOL_SET)
            for n in range(2):
                sp.dma_start(part_col[:, n:n + 1], part_row[0:1, n].rearrange("a b c d -> a (b c d)")).then_inc(part_moved, 16)

            def move_y(b, hq):
                wait(sp, pv_copied, b * HQ + (hq + 1))
                if hq == 0:
                    wait(sp, y_ready, b)
                for r in range(4):
                    row = 32 * r + D * hq
                    sp.dma_start(y_num[row:row + D, :], y_raw[32 * r:32 * r + D, hq % 2]).then_inc(y_moved[hq % 2], 16)
                    sp.dma_start(y_den[row:row + D, :], y_raw[32 * r + D:32 * r + 2 * D, hq % 2]).then_inc(y_moved[hq % 2], 16)

            def turn(it, ring):
                if on(it, lambda e: e + 1 < NB):
                    wait(sp, xn_done, (it + 1) * NT)
                    sp.dma_start(xa[:, (ring + 1) % RING], tokens(x[it + 1])).then_inc(x_loaded, 16)
                if on(it, has_c):
                    wait(sp, aux_free, aux_use(it - 1, "Cproj") + 1 if not isinstance(it, int) or it > 3 else 0)
                    for n, half in enumerate(halves(x[it - 3])):
                        sp.dma_start(xr[64 * n:64 * n + 64], half).then_inc(xr_loaded, 16)
                if on(it, has_q):
                    wait(sp, score_ready, (it - 2) * CHUNKS)
                    wait(sp, q3_done, it + 1)
                    for a, part in enumerate((q1, q2, q3)):
                        for c in range(PARTS):
                            row = (a * PARTS + c) * D
                            sp.dma_start(q_rows[ring][row:row + D],
                                         part[:, :]).then_inc(q_moved, 16)
                if on(it, has_b):
                    move_y(it - 2, 0)
                if on(it, has_q):
                    wait(sp, max_ready, (it - 2) * NSTEP)
                    wait(sp, kf_done, it + 1)
                    sp.dma_start(k_rows[ring][0:KQ, :], kf[:, :]).then_inc(k_moved, 16)
                    sp.dma_start(k_mask[ring][0:KQ, :], kf[:, :]).then_inc(k_moved, 16)
                if on(it, has_b):
                    move_y(it - 2, 1)
                    move_y(it - 2, 2)
                if on(it, has_c):
                    wait(sp, aux_free, aux_use(it, "Cffn") + 1)
                    for n, half in enumerate(halves(out[it - 3])):
                        sp.dma_start(half, o_sb[64 * n:64 * n + 64]).then_inc(o_stored, 16)
                if on(it, has_m):
                    wait(sp, aux_free, aux_use(it, "Msel") + 1)
                    for n in range(PARTS):
                        sp.dma_start(q_rows[(ring - 1) % RING][R_M + n:R_M + n + 1],
                                     m_rows[32 * n:32 * n + H, :]).then_inc(m_moved, 16)
                if on(it, has_b):
                    move_y(it - 2, 3)

            run_turns(sp, turn)
            sp.wait_ge(o_stored, 32 * NB)

        @block.tensor
        def _(pe):
            pe.wait_ge(w_loaded, 16 * N_WEIGHTS)
            pe.wait_ge(pool_set, POOL_SET)
            pe.transpose(aux_ps[0:LATENT, 0:128], wd_sb[:, :], ident[:, :]).then_inc(pe_set, 1)
            pe.wait_ge(act_set, 1)
            pe.matmul(aux_ps[:, 0:C], wdT_sb[:, :], wq_sb[:, :].rearrange("l (h d) -> l d h", d=D),
                      start=True, stop=True)
            pe.matmul(aux_ps[:, C:C + 2 * D], wdT_sb[:, :], wkv_sb[:, :], start=True, stop=True).then_inc(pe_set, 1)
            pe.wait_ge(dve_set, RING + 3)
            pe.transpose(pv_ps[:, 0:64].bitcast(BF16), wt_b[:, :], ident_b[:, :]).then_inc(pe_set, 1)
            pe.wait_ge(act_set, 2 + PARTS * PARTS + 2)

            def aux_wait(it, name):
                wait(pe, aux_free, aux_use(it, name))

            def scores(b, ring, unit):
                hq, kind = divmod(unit, 3)
                kr = k_rows[ring]

                def queries(head, j):
                    return q_rows[ring][0:K_S, head, :, 16 * j:NTILE]

                chunk0 = 5 * hq + (0, 2, 4)[kind]
                for n in range(2 if kind < 2 else 1):
                    chunk = chunk0 + n
                    wait(pe, exp_done, b * CHUNKS + (chunk - 1))
                    if unit == 0 and n == 0:
                        wait(pe, m_moved, (b + 1) * 16 * PARTS)
                    half = 2 * (chunk % 2)
                    if kind == 2:
                        for r in range(4):
                            s = pe.matmul(score_ps[:, half + r // 2, 256 * (r % 2):256 * (r % 2) + 256],
                                          kr[0:K_S, 256:384], queries(4 * hq + r, 2), start=True, stop=True)
                    else:
                        for r in (2 * n, 2 * n + 1):
                            bank = score_ps[:, half + r % 2]
                            if kind == 0:
                                s = pe.matmul(bank, kr[0:K_S, 0:128], queries(4 * hq + r, 0), start=True, stop=True)
                            else:
                                bank = bank.rearrange("p (a i) -> p a i", a=TQ)
                                pe.matmul(bank[:, :, 0:48], kr[0:K_S, 128:256], queries(4 * hq + r, 1),
                                          start=True, stop=True)
                                s = pe.matmul(bank[:, :, 48:64], kr[0:K_S, 384:512], queries(4 * hq + r, 3),
                                              start=True, stop=True)
                    s.then_inc(score_ready, 1)
                    yield

            def products(b, ring, unit):
                hq, kind = divmod(unit, 3)
                wait(pe, masked, b * MASKS + (7 * hq + (2, 6, 7)[kind]))
                if kind == 0:
                    wait(pe, pv_copied, b * HQ + hq)
                v, p = v_ones[ring], probs[kind][:, :]
                pieces = {0: [(0, 0, 64)], 1: [(1, 0, 64), (3, 48, 64)], 2: [(2, 0, 32)]}[kind]
                for j, at, pitch in pieces:
                    heads = p.rearrange("p (r a i) -> p r a i", r=4, i=pitch)
                    for r in range(4):
                        rows = pv_ps[32 * r:32 * r + 32, :].rearrange("p (a i) -> p a i", a=TQ)
                        s = pe.matmul(rows[:, :, 16 * j:NTILE], v[:, j, :],
                                      heads[:, r, :, at:at + NTILE - 16 * j],
                                      start=(kind == 0), stop=(kind == 2), skip_group_check=True)
                s.then_inc(pv_done, 1)

            def maxima(b, ring, place):
                for k in PLACES[place]:
                    g, tiles = STEPS[k]
                    wait(pe, max_done, b * NSTEP + (k - 1))
                    if k == 0:
                        wait(pe, q_moved, (b + 1) * 16 * PARTS * PARTS)
                        wait(pe, k_moved, (b + 1) * 32)
                    width = GRP * (g + 1)
                    for n, i in enumerate(tiles):
                        q_tile = q_rows[ring][0:K_MAX].rearrange("p h a i -> p (h a i)")[:, i:H * T:NTILE]
                        at = n * width
                        if g:
                            pe.matmul(max_ps[:, k % 2, at:at + width - GRP], q_tile,
                                      k_rows[ring][0:K_MAX, 0:width - GRP], start=True, stop=True)
                        s = pe.matmul(max_ps[:, k % 2, at + width - GRP:at + width], q_tile,
                                      k_mask[ring][0:K_MAX, width - GRP:width], start=True, stop=True)
                    s.then_inc(max_ready, 1)

            def turn(it, ring):
                q, m, b, c = (on(it, s) for s in (has_q, has_m, has_b, has_c))
                rm, rb = (ring - 1) % RING, (ring - 2) % RING
                for slot in range(SLOTS):
                    steps = scores(it - 2, rb, slot) if b else iter(())
                    next(steps, None)
                    if m:
                        maxima(it - 1, rm, 4 * slot)
                    next(steps, None)
                    next(steps, None)
                    if m:
                        maxima(it - 1, rm, 4 * slot + 1)
                    if slot == 0 and q:
                        wait(pe, xn_done, (it + 1) * NT)
                        aux_wait(it, "Qtr")
                        for n in range(NT):
                            s = pe.transpose(aux_ps[:, 128 * n:128 * n + 128], xn[:, n, :], ident[:, :])
                        s.then_inc(aux_filled, 1)
                    if slot == 1 and q:
                        aux_wait(it, "Qq")
                        pe.matmul(aux_ps[:, :], wdq[:, :], xnT[:, :], start=True, stop=True).then_inc(aux_filled, 1)
                    if slot == 2 and c:
                        wait(pe, y_ready, it - 2)
                        aux_wait(it, "Cproj")
                        for n in range(NT):
                            s = pe.matmul(aux_ps[:, 128 * n:128 * n + 128], yT[:, 128 * n:128 * n + 128], wp_sb[:, :],
                                          start=True, stop=True)
                        s.then_inc(aux_filled, 1)
                    if slot == 3 and q:
                        aux_wait(it, "Qk")
                        pe.matmul(aux_ps[0:KQ, :], wdk[:, :, :].rearrange("c g d -> c (g d)"), xnT[:, :],
                                  start=True, stop=True).then_inc(aux_filled, 1)
                    if slot == 4 and q:
                        aux_wait(it, "Qv")
                        for n in range(NT):
                            s = pe.matmul(aux_ps[:, D * n:D * n + D], xnT[:, 128 * n:128 * n + 128], wdv[:, :],
                                          start=True, stop=True)
                        s.then_inc(aux_filled, 1)
                    if slot == 7 and c:
                        wait(pe, xq_done, it - 2)
                        aux_wait(it, "Ctr")
                        for n in range(NT):
                            s = pe.transpose(aux_ps[:, 64 * n:64 * n + 64].bitcast(BF16), xq[:, n, :], ident_b[:, :])
                        s.then_inc(aux_filled, 1)
                    if slot == 9 and c:
                        aux_wait(it, "Cffn")
                        for n in range(NT):
                            s = pe.matmul(aux_ps[:, 128 * n:128 * n + 128], xqT[:, 128 * n:128 * n + 128], wt_T[:, :],
                                          start=True, stop=True)
                        s.then_inc(aux_filled, 1)
                    if m:
                        maxima(it - 1, rm, 4 * slot + 2)
                    if b and slot:
                        products(it - 2, rb, slot - 1)
                    if m:
                        maxima(it - 1, rm, 4 * slot + 3)
                if m:
                    wait(pe, m_split, it * 5)
                    aux_wait(it, "Msel")
                    for tl in range(TQ):
                        for n in range(PARTS):
                            s = pe.matmul(aux_ps[32 * n:32 * n + 32, NTILE * tl:NTILE * tl + NTILE], select[:, tl, :], m_parts[:, n, :],
                                          start=True, stop=True)
                    s.then_inc(aux_filled, 1)
                if b:
                    products(it - 2, rb, UNITS - 1)

            run_turns(pe, turn)

        @block.scalar
        def _(act):
            act.wait_ge(pe_set, 1)
            act.copy(wdT_sb[:, :], aux_ps[0:LATENT, 0:128]).then_inc(act_set, 1)
            act.wait_ge(pe_set, 2)
            act.copy(wdq[:, :], aux_ps[:, 0:C]).then_inc(act_set, 1)
            for g in range(PARTS * PARTS):
                act.copy(wdk[:, g, :], aux_ps[:, C:C + D]).then_inc(act_set, 1)
            act.copy(wdv[:, :], aux_ps[:, C + D:C + 2 * D]).then_inc(act_set, 1)
            act.wait_ge(pe_set, 3)
            act.copy(wt_T[:, :], pv_ps[:, 0:64].bitcast(BF16)).then_inc(act_set, 1)
            act.wait_ge(part_moved, 32)

            def exps(b, unit):
                hq, kind = divmod(unit, 3)
                for n in range(2 if kind < 2 else 1):
                    chunk = 5 * hq + (0, 2, 4)[kind] + n
                    wait(act, score_ready, b * CHUNKS + (chunk + 1))
                    if n == 0:
                        wait(act, pv_done, b * UNITS + (unit - 2))
                    half = 2 * (chunk % 2)
                    act.activation(probs[kind][:, 1024 * n:1024 * n + 1024],
                                   score_ps[:, half:half + 2].rearrange("p a b -> p (a b)"),
                                   ACT.Exp, scale=SCALE).then_inc(exp_done, 1)

            def copy_products(b, hq):
                wait(act, pv_done, b * UNITS + 3 * (hq + 1))
                wait(act, y_moved[hq % 2], (b * (HQ // 2) + hq // 2) * Y_MOVES)
                act.copy(y_raw[:, hq % 2], pv_ps[:, :]).then_inc(pv_copied, 1)

            def turn(it, ring):
                q, m, b, c = (on(it, s) for s in (has_q, has_m, has_b, has_c))
                for slot in range(SLOTS):
                    if b:
                        exps(it - 2, slot)
                    if slot == 0 and q:
                        wait(act, aux_filled, aux_use(it, "Qtr") + 1)
                        act.copy(xnT[:, :], aux_ps[:, :]).then_inc(aux_free, 1)
                    if slot == 1 and q:
                        wait(act, aux_filled, aux_use(it, "Qq") + 1)
                        wait(act, q_moved, it * 16 * PARTS * PARTS)
                        act.copy(positions(q1), by_position(aux_ps)).then_inc(q1_done, 1)
                    if slot == 3 and q:
                        wait(act, aux_filled, aux_use(it, "Qk") + 1)
                        act.activation(k1[:, :], aux_ps[0:KQ, :], ACT.Copy, scale=part_col[:, 0:1]).then_inc(k1_done, 1)
                    if slot == 7 and c:
                        wait(act, aux_filled, aux_use(it, "Ctr") + 1)
                        act.copy(xqT[:, :], aux_ps[:, 0:256].bitcast(BF16)).then_inc(aux_free, 1)
                    if b and slot % 3 == 0 and slot:
                        copy_products(it - 2, slot // 3 - 1)
                if m:
                    wait(act, aux_filled, aux_use(it, "Msel") + 1)
                    wait(act, m_moved, (it - 1) * 16 * PARTS)
                    act.copy(m_rows[:, :], aux_ps[0:32 * PARTS, :]).then_inc(aux_free, 1)
                if b:
                    copy_products(it - 2, HQ - 1)

            run_turns(act, turn)

        @block.vector
        def _(dve):
            for n in range(RING):
                dve.memset(v_ones[n][:, :, :], 1.0).then_inc(dve_set, 1)
            dve.wait_ge(dve_set, RING)
            dve.wait_ge(w_loaded, 16 * N_WEIGHTS)
            dve.tensor_scalar(scale_sb[:, 1:2], scale_sb[:, 0:1], EPS, None, ALU.max).then_inc(dve_set, 1)
            dve.wait_ge(dve_set, RING + 1)
            dve.reciprocal(scale_sb[:, 2:3], scale_sb[:, 1:2]).then_inc(dve_set, 1)
            dve.tensor_scalar(wt_b[:, :], wt_i[:, :], -1.0, None, ALU.add).then_inc(dve_set, 1)
            dve.tensor_scalar(scale_sb[:, 3:4], scale_sb[:, 1:2], BIGGEST, None, ALU.min).then_inc(dve_set, 1)
            dve.wait_ge(dve_set, RING + 4)

            def moments(src, st, mv, b, stats, aggr):
                for n in range(NT):
                    dve.bn_stats(st[:, n, :], src[:, n, :]).then_inc(stats, 1)
                wait(dve, stats, (b + 1) * NT)
                apart(dve, b)
                for n in range(NT):
                    dve.bn_aggr(mv[:, n, :], st[:, n, :]).then_inc(aggr, 1)

            def moments1(b, ring):
                wait(dve, x_loaded, (b + 1) * 16)
                wait(dve, xn_done, b * NT)
                moments(xa[:, ring], st1, mv1, b, ln1_stats, ln1_aggr)

            def maxima(b, place):
                for k in PLACES[place]:
                    g, tiles = STEPS[k]
                    wait(dve, max_ready, b * NSTEP + (k + 1))
                    if k == 0:
                        wait(dve, m_split, b * 5)
                    n = len(tiles)
                    width = GRP * (g + 1)
                    src = max_ps[:, k % 2, 0:n * width].rearrange("p (n w) -> p n w", n=n)
                    dve.tensor_reduce(neg_max[:, tiles[0]:tiles[0] + n], src, AX_X, ALU.max,
                                      negate=True).then_inc(max_done, 1)

            def turn(it, ring):
                q, m, b, c = (on(it, s) for s in (has_q, has_m, has_b, has_c))
                for slot in range(SLOTS):
                    if slot == 0 and c:
                        for n in range(2):
                            wait(dve, y_moved[n], (it - 2) * (HQ // 2) * Y_MOVES)
                        wait(dve, y_ready, it - 3)
                        dve.reciprocal(y_inv[:, :], y_den[:, :]).then_inc(inv_done, 1)
                    if m:
                        for n in range(4):
                            maxima(it - 1, 4 * slot + n)
                    if slot == 1 and q:
                        wait(dve, q1_done, it + 1)
                        wait(dve, q3_done, it)
                        dve.tensor_tensor(positions(q_r), by_position(aux_ps), positions(q1), ALU.subtract).then_inc(aux_free, 1)
                    if slot == 2 and c:
                        wait(dve, aux_filled, aux_use(it, "Cproj") + 1)
                        wait(dve, xr_loaded, (it - 2) * 32)
                        wait(dve, x1b_done, it - 3)
                        wait(dve, z_step, (it - 3) * (NT + 5))
                        dve.tensor_tensor(x1[:, :, :], aux_ps[:, :].rearrange("p (n c) -> p n c", n=NT), xr[:, :, :],
                                          ALU.add).then_inc(aux_free, 1)
                        wait(dve, aux_free, aux_use(it, "Cproj") + 1)
                        moments(x1, st2, mv2, it - 3, ln2_stats, ln2_aggr)
                    if slot == 3 and q:
                        wait(dve, k1_done, it + 1)
                        wait(dve, kf_done, it)
                        dve.tensor_tensor(k_r[:, :], aux_ps[0:KQ, :], k1[:, :], ALU.subtract).then_inc(aux_free, 1)
                    if slot == 4 and q:
                        wait(dve, aux_filled, aux_use(it, "Qv") + 1)
                        wait(dve, pv_done, (it - 2) * UNITS)
                        dve.tensor_copy(v_ones[ring][:, :, 0:D],
                                        aux_ps[:, 0:NT * D].rearrange("p (n d) -> p n d", n=NT)).then_inc(aux_free, 1)
                    if slot == 5 and on(it, lambda e: e + 1 < NB):
                        moments1(it + 1, (ring + 1) % RING)
                    if slot == 9 and c:
                        wait(dve, aux_filled, aux_use(it, "Cffn") + 1)
                        wait(dve, x1b_done, it - 2)
                        wait(dve, o_stored, (it - 3) * 32)
                        dve.scalar_tensor_tensor(out=o_sb[:, :, :].rearrange("p n c -> p (n c)"), in0=aux_ps[:, :],
                                                 scalar=scale_sb[:, 3:4],
                                                 in1=x1b[:, :, :].rearrange("p n c -> p (n c)"),
                                                 op0=ALU.mult, op1=ALU.add).then_inc(aux_free, 1)
                if m:
                    wait(dve, max_done, it * NSTEP)
                    if not isinstance(it, int) or it > 1:
                        wait(dve, aux_filled, aux_use(it - 1, "Msel") + 1)
                    dve.tensor_copy(m_parts[:, 0, :], neg_max[:, :]).then_inc(m_split, 1)
                    wait(dve, m_split, it * 5 - 4)
                    dve.tensor_tensor(m_r[:, 0, :], neg_max[:, :], m_parts[:, 0, :], ALU.subtract).then_inc(m_split, 1)
                    wait(dve, m_split, it * 5 - 3)
                    dve.tensor_copy(m_parts[:, 1, :], m_r[:, 0, :]).then_inc(m_split, 1)
                    wait(dve, m_split, it * 5 - 2)
                    dve.tensor_tensor(m_r[:, 1, :], m_r[:, 0, :], m_parts[:, 1, :], ALU.subtract).then_inc(m_split, 1)
                    wait(dve, m_split, it * 5 - 1)
                    dve.tensor_copy(m_parts[:, 2, :], m_r[:, 1, :]).then_inc(m_split, 1)

            moments1(0, 0)
            run_turns(dve, turn)

        @block.gpsimd
        def _(pool):
            count = [0]

            def done(ins):
                ins.then_inc(pool_set, 1)
                count[0] += 1
                pool.wait_ge(pool_set, count[0])

            done(pool.memset(ident[:, :], 0.0))
            done(pool.memset(ident_b[:, :], 0.0))
            done(pool.memset(select[:, :, :], 0.0))
            done(pool.memset(part_row[:, :, :, :, :], 0.0))
            done(pool.memset(half_neg[:, :], -0.5))
            done(pool.affine_select(out=ident[:, :], in_=ident[:, :], compare_op=ALU.not_equal, fill=1.0, base=0,
                                    pattern=[[-1, 128]], channel_multiplier=1))
            done(pool.affine_select(out=ident_b[:, :], in_=ident_b[:, :], compare_op=ALU.not_equal, fill=1.0, base=0,
                                    pattern=[[-1, 128]], channel_multiplier=1))
            done(pool.affine_select(out=select[:, :, :], in_=select[:, :, :], compare_op=ALU.not_equal, fill=1.0,
                                    base=0, pattern=[[-1, TQ], [-TQ, 32]], channel_multiplier=1))
            done(pool.memset(part_row[:, 0, :, 1:3, :], 1.0))
            done(pool.memset(part_row[:, 1, :, 2:3, :], 1.0))
            for n in range(RING):
                done(pool.memset(q_rows[n][64:128, :, :], 0.0))
                one_hot = q_rows[n][64:96].rearrange("p h a (g b) -> p h a g b", b=GRP // TQ)
                for h in range(H):
                    last = pool.affine_select(out=one_hot[:, h], in_=one_hot[:, h], compare_op=ALU.not_equal,
                                              fill=1.0, base=R_MASK - 64,
                                              pattern=[[1, TQ], [0, T // GRP], [TQ, GRP // TQ]],
                                              channel_multiplier=-1)
                done(last)
                done(pool.memset(k_rows[n][64:96, :], 0.0))
                done(pool.memset(k_rows[n][96:128, :], 1.0))
                done(pool.memset(k_mask[n][64:96, :], 0.0))
                done(pool.memset(k_mask[n][96:128, :], 0.0))
                done(pool.affine_select(out=k_mask[n][64:96, :].rearrange("p (g t) -> p g t", t=GRP),
                                        in_=k_mask[n][64:96, :].rearrange("p (g t) -> p g t", t=GRP),
                                        compare_op=ALU.is_ge, fill=NEG, base=-(R_MASK - 64),
                                        pattern=[[0, T // GRP], [-1, GRP]], channel_multiplier=1))
            assert count[0] == POOL_SET

            def small_ln(mv, ln, step, b, per, aggr):
                wait(pool, aggr, (b + 1) * NT)
                apart(pool, b)
                pool.tensor_scalar(ln[:, 0, :], mv[:, :, 1], EPS, 1.0, ALU.add, ALU.mult).then_inc(step, 1)
                pool.tensor_scalar(ln[:, 1, :], mv[:, :, 0], -1.0, 0.0, ALU.mult, ALU.add).then_inc(step, 1)
                wait(pool, step, b * per + 2)
                pool.tensor_tensor(ln[:, 2, :], ln[:, 0, :], half_neg[:, :], ALU.pow).then_inc(step, 1)
                wait(pool, step, b * per + 3)
                apart(pool, b)

            def norm1(b, ring):
                small_ln(mv1, ln1, ln1_step, b, 4, ln1_aggr)
                pool.tensor_tensor(ln1[:, 3, :], ln1[:, 1, :], ln1[:, 2, :], ALU.mult).then_inc(ln1_step, 1)
                wait(pool, ln1_step, (b + 1) * 4)
                apart(pool, b)
                for n in range(NT):
                    pool.tensor_scalar(xn[:, n, :], xa[:, ring, n, :], ln1[:, 2, n:n + 1], ln1[:, 3, n:n + 1],
                                       ALU.mult, ALU.add).then_inc(xn_done, 1)

            def select_causal(b, unit):
                hq, kind = divmod(unit, 3)
                for n in range(2 if kind < 2 else 1):
                    chunk = 5 * hq + (0, 2, 4)[kind] + n
                    wait(pool, exp_done, b * CHUNKS + (chunk + 1))
                    apart(pool, b)
                    p = probs[kind][:, 1024 * n:1024 * n + 1024]
                    tiles = p.rearrange("p (ra i) -> p ra i", i=32 if kind == 2 else 64)
                    for at in {0: [0], 1: [0, 48], 2: [0]}[kind]:
                        v = tiles[:, :, at:at + 16]
                        pool.affine_select(out=v, in_=v, compare_op=ALU.is_ge, fill=0.0, base=0,
                                           pattern=[[0, 4 if kind == 2 else 2], [1, TQ], [TQ, 16]],
                                           channel_multiplier=-1).then_inc(masked, 1)

            def quantise(b):
                small_ln(mv2, ln2, ln2_step, b, 5, ln2_aggr)
                pool.tensor_scalar(ln2[:, 4, :], ln2[:, 2, :], scale_sb[:, 2:3], 0.0, ALU.mult, ALU.add).then_inc(ln2_step, 1)
                wait(pool, ln2_step, b * 5 + 4)
                pool.tensor_tensor(ln2[:, 3, :], ln2[:, 1, :], ln2[:, 4, :], ALU.mult).then_inc(ln2_step, 1)
                wait(pool, ln2_step, (b + 1) * 5)
                apart(pool, b)
                zs = b * (NT + 5)
                for n in range(NT):
                    pool.tensor_scalar(z[:, n, :], x1[:, n, :], ln2[:, 4, n:n + 1], ln2[:, 3, n:n + 1],
                                       ALU.mult, ALU.add).then_inc(z_step, 1)
                wait(pool, z_step, zs + NT)
                apart(pool, b)
                pool.tensor_scalar(z_neg[:, :, :], z[:, :, :], -1.0, 0.0, ALU.mult, ALU.add).then_inc(z_step, 1)
                pool.tensor_scalar(z_lo[:, :, :], z[:, :, :], QB, -QB, ALU.min, ALU.max).then_inc(z_step, 1)
                wait(pool, z_step, zs + NT + 2)
                apart(pool, b)
                pool.tensor_scalar(z[:, :, :], z_neg[:, :, :], QB, -QB, ALU.min, ALU.max).then_inc(z_step, 1)
                wait(pool, z_step, zs + NT + 3)
                pool.tensor_tensor(z_neg[:, :, :], z_lo[:, :, :], z[:, :, :], ALU.subtract).then_inc(z_step, 1)
                wait(pool, z_step, zs + NT + 4)
                apart(pool, b)
                pool.tensor_scalar(z_lo[:, :, :], z_neg[:, :, :], 0.5, ROUND, ALU.mult, ALU.add).then_inc(z_step, 1)
                wait(pool, z_step, zs + NT + 5)
                apart(pool, b)
                pool.tensor_scalar(xq[:, :, :], z_lo[:, :, :], -ROUND, 1.0, ALU.add, ALU.mult).then_inc(xq_done, 1)

            pool.wait_ge(w_loaded, 16 * N_WEIGHTS)
            pool.wait_ge(part_moved, 32)
            pool.wait_ge(dve_set, RING + 4)
            norm1(0, 0)

            def turn(it, ring):
                q, m, b, c = (on(it, s) for s in (has_q, has_m, has_b, has_c))
                for slot in range(SLOTS):
                    if b:
                        select_causal(it - 2, slot)
                    if slot == 0 and c:
                        wait(pool, inv_done, it - 2)
                        if not isinstance(it, int) or it > 3:
                            wait(pool, aux_filled, aux_use(it - 1, "Cproj") + 1)
                        for n in range(2):
                            wait(pool, y_moved[n], (it - 2) * (HQ // 2) * Y_MOVES)
                        pool.tensor_tensor(yT[:, :], y_num[:, :], y_inv[:, :], ALU.mult).then_inc(y_ready, 1)
                    if slot == 1 and q:
                        wait(pool, aux_free, aux_use(it, "Qq") + 1)
                        wait(pool, q_moved, it * 16 * PARTS * PARTS)
                        apart(pool, it)
                        pool.tensor_scalar(q2[:, :], q_r[:, :], 1.0, 0.0, ALU.mult, ALU.add).then_inc(q2_done, 1)
                        wait(pool, q2_done, it + 1)
                        pool.tensor_tensor(q3[:, :], q_r[:, :], q2[:, :], ALU.subtract).then_inc(q3_done, 1)
                    if slot == 3 and q:
                        wait(pool, aux_free, aux_use(it, "Qk") + 1)
                        wait(pool, k_moved, it * 32)
                        apart(pool, it)
                        pool.tensor_scalar(k2[:, :], k_r[:, :], part_col[:, 1:2], 0.0, ALU.mult, ALU.add).then_inc(k2_done, 1)
                        wait(pool, k2_done, it + 1)
                        pool.tensor_tensor(kf[:, :], k_r[:, :], k2[:, :], ALU.subtract).then_inc(kf_done, 1)
                    if slot == 4 and c:
                        quantise(it - 3)
                        if not isinstance(it, int) or it > 3:
                            wait(pool, aux_free, aux_use(it - 1, "Cffn") + 1)
                        pool.tensor_tensor(x1b[:, :, :], x1[:, :, :],
                                           bias_sb[:, :].rearrange("p (a c) -> p a c", a=1).broadcast_to([128, NT, C]),
                                           ALU.add).then_inc(x1b_done, 1)
                    if slot == 6 and on(it, lambda e: e + 1 < NB):
                        wait(pool, aux_filled, aux_use(it, "Qtr") + 1)
                        norm1(it + 1, (ring + 1) % RING)

            run_turns(pool, turn)


_INS = ["L0_attn_x", "L0_attn_Wc_down", "L0_attn_Wq_up", "L0_attn_Wkv_up", "L0_attn_Wc_proj",
        "L0_ffn_ternary_weight", "L0_ffn_bias", "L0_ffn_act_scale"]


def kernel(**inputs):
    import numpy as _np
    import concourse.bacc as _bacc
    from concourse import mybir as _mybir
    from concourse.bass_utils import run_bass_kernel_spmd as _run

    nc = _bacc.Bacc("TRN2", target_bir_lowering=False, num_devices=1)
    arrays, args = {}, []
    for name in _INS:
        a = _np.ascontiguousarray(inputs[name])
        if name == "L0_ffn_act_scale":
            a = a.reshape(1, 1)
        arrays[f"in_{name}_dram"] = a
        args.append(nc.dram_tensor(f"in_{name}_dram", a.shape, _mybir.dt.from_np(a.dtype), kind="ExternalInput").ap())
    args.append(nc.dram_tensor("out_dram", (NB, T, C), _mybir.dt.float32, kind="ExternalOutput").ap())
    program(nc, *args)
    r = _run(nc, [arrays], core_ids=[0])
    return r.results[0]["out_dram"]
```

```python
from contextlib import ExitStack

import concourse.bass as bass
from concourse import mybir

F32 = mybir.dt.float32
BF16 = mybir.dt.bfloat16
I32 = mybir.dt.int32
ALU = mybir.AluOpType
ACT = mybir.ActivationFunctionType
AX_X = mybir.AxisListType.X

NB, T, C = 16, 512, 128
H, D = 16, 8
LATENT = 64
NT = T // 128
PARTS = 3
KQ = PARTS * PARTS * D
GRP = 16
R_MASK = KQ
K_MAX = 96
R_M = 96
K_S = R_M + PARTS
TQ = 8
NTILE = T // TQ
NEG = -1.0e38
SCALE = 1.0 / float(D) ** 0.5
EPS = 1e-5
QB = 127.0
ROUND = 12582912.0
BIGGEST = 3.0e38
RING = 3

HQ = 4
MASKS = 16
CHUNKS = 20
UNITS = 12
SLOTS = UNITS
MAX_FROM, MAX_TO = 2, 46
B_LATE = 2
STEPS = [(g, (2 * g, 2 * g + 1)) for g in range(16)] + [(i // 2, (i,)) for i in range(32, NTILE)]
NSTEP = len(STEPS)


def step_places():
    cost = [len(tiles) * GRP * (g + 1) + 100 for g, tiles in STEPS]
    total, at, out = sum(cost), 0, [[] for _ in range(4 * SLOTS)]
    for k, c in enumerate(cost):
        out[MAX_FROM + int((at + c / 2) * (MAX_TO - MAX_FROM) / total)].append(k)
        at += c
    return out


PLACES = step_places()

def has_q(it): return 0 <= it < NB
def has_m(it): return 0 <= it - 1 < NB
def has_b(it): return 0 <= it - 2 < NB
def has_next(it): return 0 <= it + 1 < NB
def has_c(it): return 0 <= it - 3 < NB

FIRST_TURN, LAST_TURN = -1, NB + 3
STEADY = (3, NB - 1)
AUX = [("Msel", has_b), ("Qk", has_q), ("Qq", has_q), ("Yb", has_c), ("Yt", has_c), ("Cproj", has_c),
       ("Qv", has_q), ("Qtr", has_next), ("Ctr", has_c), ("Cffn", has_c), ("Ya", has_b)]


def aux_use(it, name):
    if isinstance(it, int):
        before = sum(on(e) for e in range(FIRST_TURN, it) for _, on in AUX)
        for n, on in AUX:
            if n == name:
                return before
            before += on(it)
    start = sum(on(e) for e in range(FIRST_TURN, STEADY[0]) for _, on in AUX)
    return (it - STEADY[0]) * len(AUX) + (start + [n for n, _ in AUX].index(name))


def head_of(hq, r):
    return 8 * (hq // 2) + 2 * r + hq % 2


def wait(eng, sem, value):
    if not isinstance(value, int) or value > 0:
        eng.wait_ge(sem, value)


def program(nc, x, w_down, w_q, w_kv, w_proj, w_tern, bias, act_scale, out):
    with ExitStack() as ctx:
        def sb(name, shape, dt):
            return ctx.enter_context(nc.sbuf_tensor(name, shape, dt))

        def sem(name):
            return ctx.enter_context(nc.semaphore(name))

        score_ps = ctx.enter_context(nc.psum_tensor("score_ps", [128, 4, 512], F32))
        pv_ps = ctx.enter_context(nc.psum_tensor("pv_ps", [128, 512], F32))
        max_ps = ctx.enter_context(nc.psum_tensor("max_ps", [128, 2, 512], F32))
        aux_ps = ctx.enter_context(nc.psum_tensor("aux_ps", [128, 512], F32))

        ident = sb("ident", [128, 128], F32)
        ident_b = sb("ident_b", [128, 128], BF16)
        select = sb("select", [128, TQ, 80], BF16)
        half_neg = sb("half_neg", [128, NT], F32)
        part_row = sb("part_row", [1, 2, PARTS, PARTS, D], F32)
        part_col = sb("part_col", [KQ, 2], F32)
        wd_sb = sb("wd_sb", [128, LATENT], F32)
        wdT_sb = sb("wdT_sb", [LATENT, 128], F32)
        wq_sb = sb("wq_sb", [LATENT, C], F32)
        wkv_sb = sb("wkv_sb", [LATENT, 2 * D], F32)
        wdq = sb("wdq", [128, C], F32)
        wdk = sb("wdk", [128, PARTS * PARTS, D], F32)
        wdv = sb("wdv", [128, D], F32)
        wp_sb = sb("wp_sb", [128, C], F32)
        wt_i = sb("wt_i", [128, C], I32)
        wt_b = sb("wt_b", [128, C], BF16)
        wt_T = sb("wt_T", [128, C], BF16)
        bias_sb = sb("bias_sb", [128, C], F32)
        scale_sb = sb("scale_sb", [128, 4], F32)

        xa = sb("xa", [128, RING, NT, C], F32)
        st1 = sb("st1", [128, NT, 6], F32)
        mv1 = sb("mv1", [128, NT, 2], F32)
        ln1 = sb("ln1", [128, 4, NT], F32)
        xn = sb("xn", [128, NT, C], F32)
        xnT = sb("xnT", [128, T], F32)
        q1 = sb("q1", [128, T], BF16)
        q_r = sb("q_r", [128, T], F32)
        q2 = sb("q2", [128, T], BF16)
        q3 = sb("q3", [128, T], BF16)
        k1 = sb("k1", [KQ, T], BF16)
        k_r = sb("k_r", [KQ, T], F32)
        k2 = sb("k2", [KQ, T], BF16)
        kf = sb("kf", [KQ, T], BF16)
        one_hot = sb("one_hot", [128, TQ, NTILE], BF16)
        q_rows = [sb(f"q_rows{n}", [128, H, TQ, NTILE], BF16) for n in range(RING)]
        k_rows = [sb(f"k_rows{n}", [128, T], BF16) for n in range(RING)]
        k_mask = [sb(f"k_mask{n}", [128, T], BF16) for n in range(RING)]
        v_ones = [sb(f"v_ones{n}", [128, NT, 2, 32], F32) for n in range(RING)]
        neg_max = sb("neg_max", [128, NTILE], F32)
        m_r = sb("m_r", [128, 2, NTILE], F32)
        m_parts = sb("m_parts", [128, PARTS, NTILE], BF16)
        m_rows = sb("m_rows", [H * PARTS, T], BF16)
        probs = [sb(f"probs{n}", [128, w], F32) for n, w in enumerate((2048, 2048, 1024))]
        y_raw = sb("y_raw", [128, 2, T], F32)
        y_inv = sb("y_inv", [128, NT * H // 2], F32)
        y_t = sb("y_t", [128, NT, C], F32)
        yT = sb("yT", [128, T], F32)
        xr = sb("xr", [128, NT, C], F32)
        x1 = sb("x1", [128, NT, C], F32)
        x1b = sb("x1b", [128, NT, C], F32)
        st2 = sb("st2", [128, NT, 6], F32)
        mv2 = sb("mv2", [128, NT, 2], F32)
        ln2 = sb("ln2", [128, 5, NT], F32)
        z = sb("z", [128, NT, C], F32)
        z_up = sb("z_up", [128, NT, C], F32)
        zb = sb("zb", [128, NT, C], BF16)
        z_lo = sb("z_lo", [128, NT, C], BF16)
        z_hi = sb("z_hi", [128, NT, C], BF16)
        xq = sb("xq", [128, NT, C], BF16)
        xqT = sb("xqT", [128, T], BF16)
        o_sb = sb("o_sb", [128, NT, C], F32)

        w_loaded = sem("w_loaded")
        pool_set = sem("pool_set")
        dve_set = sem("dve_set")
        act_set = sem("act_set")
        pe_set = sem("pe_set")
        part_moved = sem("part_moved")
        hot_moved = sem("hot_moved")
        x_loaded = sem("x_loaded")
        ln1_stats = sem("ln1_stats")
        ln1_aggr = sem("ln1_aggr")
        ln1_step = sem("ln1_step")
        xn_done = sem("xn_done")
        aux_filled = sem("aux_filled")
        aux_free = sem("aux_free")
        q1_done = sem("q1_done")
        q2_done = sem("q2_done")
        q3_done = sem("q3_done")
        k1_done = sem("k1_done")
        k2_done = sem("k2_done")
        kf_done = sem("kf_done")
        q_moved = sem("q_moved")
        k_moved = sem("k_moved")
        max_ready = sem("max_ready")
        max_done = sem("max_done")
        m_split = sem("m_split")
        m_moved = sem("m_moved")
        score_ready = sem("score_ready")
        exp_done = sem("exp_done")
        masked = sem("masked")
        pv_done = sem("pv_done")
        pv_copied = sem("pv_copied")
        inv_done = sem("inv_done")
        xr_loaded = sem("xr_loaded")
        ln2_stats = sem("ln2_stats")
        ln2_aggr = sem("ln2_aggr")
        ln2_step = sem("ln2_step")
        z_step = sem("z_step")
        zb_done = sem("zb_done")
        clipped = sem("clipped")
        xq_done = sem("xq_done")
        x1b_done = sem("x1b_done")
        o_stored = sem("o_stored")

        carried = sem("carried")

        N_WEIGHTS = 7
        HOT_SET = 10
        POOL_SET = HOT_SET + 2 + 4 * RING

        def tokens(dram):
            return dram.rearrange("(n p) c -> p n c", p=128)

        def halves(dram):
            v = dram.rearrange("(i n a) c -> a i n c", n=NT, a=2)
            return v[0], v[1]

        def apart(eng, value):
            if not isinstance(value, int):
                eng.sem_inc(carried, 1)

        def positions(a):
            return a[:, :].rearrange("p (a i) -> p a i", a=TQ)

        def by_position(a):
            return a[:, :].rearrange("p (i a) -> p a i", a=TQ)

        def run_turns(eng, turn):
            for it in range(FIRST_TURN, STEADY[0]):
                turn(it, it % RING)
            with eng.Fori(0, (STEADY[1] - STEADY[0]) // RING) as i:
                for u in range(RING):
                    turn(i * RING + (STEADY[0] + u), (STEADY[0] + u) % RING)
            for it in range(STEADY[1], LAST_TURN):
                turn(it, it % RING)

        def on(it, stage):
            return stage(it) if isinstance(it, int) else True

        block = ctx.enter_context(nc.Block())

        @block.sync
        def _(sp):
            sp.dma_start(wd_sb[:, :], w_down).then_inc(w_loaded, 16)
            sp.dma_start(wq_sb[:, :], w_q).then_inc(w_loaded, 16)
            sp.dma_start(wkv_sb[:, :], w_kv).then_inc(w_loaded, 16)
            sp.dma_start(wt_i[:, :], w_tern).then_inc(w_loaded, 16)
            sp.dma_start(bias_sb[:, :], bias.rearrange("(a c) -> a c", a=1).broadcast_to([128, C])).then_inc(w_loaded, 16)
            sp.dma_start(scale_sb[:, 0:1], act_scale.broadcast_to([128, 1])).then_inc(w_loaded, 16)
            sp.dma_start(wp_sb[:, :], w_proj).then_inc(w_loaded, 16)
            sp.wait_ge(pool_set, HOT_SET)
            for n in range(2):
                sp.dma_start(part_col[:, n:n + 1], part_row[0:1, n].rearrange("a b c d -> a (b c d)")).then_inc(part_moved, 16)
            for n in range(RING):
                sp.dma_start(q_rows[n][64:96].rearrange("p h a i -> p h (a i)"),
                             one_hot[64:96].rearrange("p (h a) i -> p h (a i)", h=1).broadcast_to([32, H, T])).then_inc(hot_moved, 16)
            sp.wait_ge(pool_set, POOL_SET)
            sp.wait_ge(hot_moved, 16 * RING)

            def turn(it, ring):
                if on(it, has_next):
                    wait(sp, xn_done, (it + 1) * NT)
                    sp.dma_start(xa[:, (ring + 1) % RING], tokens(x[it + 1])).then_inc(x_loaded, 16)
                if on(it, has_b):
                    wait(sp, aux_free, aux_use(it, "Msel") + 1)
                    sp.dma_start(q_rows[(ring - 2) % RING][R_M:R_M + PARTS], m_rows[:, :]).then_inc(m_moved, 16)
                if on(it, has_c):
                    if not isinstance(it, int) or it > 3:
                        wait(sp, aux_free, aux_use(it - 1, "Cproj") + 1)
                    for n, half in enumerate(halves(x[it - 3])):
                        sp.dma_start(xr[64 * n:64 * n + 64], half).then_inc(xr_loaded, 16)
                if on(it, has_q):
                    wait(sp, score_ready, (it - 2) * CHUNKS)
                    wait(sp, kf_done, it + 1)
                    sp.dma_start(k_rows[ring][0:KQ, :], kf[:, :]).then_inc(k_moved, 16)
                    wait(sp, max_ready, (it - 2) * NSTEP)
                    sp.dma_start(k_mask[ring][0:KQ, :], kf[:, :]).then_inc(k_moved, 16)
                    wait(sp, q3_done, it + 1)
                    for a, part in enumerate((q1, q2, q3)):
                        for g in range(PARTS):
                            row = (a * PARTS + g) * D
                            sp.dma_start(q_rows[ring][row:row + D], part[:, :]).then_inc(q_moved, 16)
                if on(it, has_c):
                    wait(sp, aux_free, aux_use(it, "Cffn") + 1)
                    for n, half in enumerate(halves(out[it - 3])):
                        sp.dma_start(half, o_sb[64 * n:64 * n + 64]).then_inc(o_stored, 16)

            sp.sem_inc(o_stored, 32)
            run_turns(sp, turn)
            sp.wait_ge(o_stored, 32 * (NB + 1))

        @block.tensor
        def _(pe):
            pe.wait_ge(w_loaded, 16 * N_WEIGHTS)
            pe.wait_ge(pool_set, 4)
            pe.transpose(aux_ps[0:LATENT, 0:128], wd_sb[:, :], ident[:, :]).then_inc(pe_set, 1)
            pe.wait_ge(act_set, 1)
            pe.matmul(aux_ps[:, 0:C], wdT_sb[:, :], wq_sb[:, :].rearrange("l (h d) -> l d h", d=D),
                      start=True, stop=True)
            pe.matmul(aux_ps[:, C:C + 2 * D], wdT_sb[:, :], wkv_sb[:, :], start=True, stop=True).then_inc(pe_set, 1)
            pe.wait_ge(dve_set, 3 * RING + 3)
            pe.transpose(pv_ps[:, 0:64].bitcast(BF16), wt_b[:, :], ident_b[:, :]).then_inc(pe_set, 1)
            pe.wait_ge(act_set, 2 + PARTS * PARTS + 2)
            pe.wait_ge(pool_set, POOL_SET)

            def aux_wait(it, name):
                wait(pe, aux_free, aux_use(it, name))

            def scores(b, ring, unit):
                hq, kind = divmod(unit, 3)
                kr = k_rows[ring]

                def queries(head, j):
                    return q_rows[ring][0:K_S, head, :, 16 * j:NTILE]

                chunk0 = 5 * hq + (0, 2, 4)[kind]
                for n in range(2 if kind < 2 else 1):
                    chunk = chunk0 + n
                    wait(pe, exp_done, b * CHUNKS + (chunk - 1))
                    if unit == 0 and n == 0:
                        wait(pe, m_moved, (b + 1) * 16)
                    half = 2 * (chunk % 2)
                    if kind == 2:
                        for r in range(4):
                            s = pe.matmul(score_ps[:, half + r // 2, 256 * (r % 2):256 * (r % 2) + 256],
                                          kr[0:K_S, 256:384], queries(head_of(hq, r), 2), start=True, stop=True)
                    else:
                        for r in (2 * n, 2 * n + 1):
                            bank = score_ps[:, half + r % 2]
                            if kind == 0:
                                s = pe.matmul(bank, kr[0:K_S, 0:128], queries(head_of(hq, r), 0), start=True, stop=True)
                            else:
                                bank = bank.rearrange("p (a i) -> p a i", a=TQ)
                                pe.matmul(bank[:, :, 0:48], kr[0:K_S, 128:256], queries(head_of(hq, r), 1),
                                          start=True, stop=True)
                                s = pe.matmul(bank[:, :, 48:64], kr[0:K_S, 384:512], queries(head_of(hq, r), 3),
                                              start=True, stop=True)
                    s.then_inc(score_ready, 1)
                    yield

            def products(b, ring, unit):
                hq, kind = divmod(unit, 3)
                wait(pe, masked, b * MASKS + (4 * hq + (1, 3, 4)[kind]))
                if kind == 0 and hq % 2 == 0:
                    wait(pe, pv_copied, b * 2 + hq // 2)
                v, p = v_ones[ring], probs[kind][:, :]
                pieces = {0: [(0, 0, 64)], 1: [(1, 0, 64), (3, 48, 64)], 2: [(2, 0, 32)]}[kind]
                for j, at, pitch in pieces:
                    heads = p.rearrange("p (r a i) -> p r a i", r=4, i=pitch)
                    for r in range(4):
                        rows = pv_ps[32 * r:32 * r + 32, :].rearrange("p (a i) -> p a i", a=TQ)
                        s = pe.matmul(rows[:, :, 16 * j:NTILE], v[:, j, hq % 2, :],
                                      heads[:, r, :, at:at + NTILE - 16 * j],
                                      start=(kind == 0 and hq % 2 == 0), stop=(kind == 2 and hq % 2 == 1), skip_group_check=True)
                s.then_inc(pv_done, 1)

            def turn_products(it, pair, name, b):
                wait(pe, pv_copied, b * 2 + (pair + 1))
                aux_wait(it, name)
                for n in range(NT):
                    s = pe.transpose(aux_ps[:, 128 * n:128 * n + 128], y_raw[:, pair, 128 * n:128 * n + 128], ident[:, :])
                s.then_inc(aux_filled, 1)

            def maxima(b, ring, place):
                for k in PLACES[place]:
                    g, tiles = STEPS[k]
                    wait(pe, max_done, b * NSTEP + (k - 1))
                    if k == 0:
                        wait(pe, q_moved, (b + 1) * 16 * PARTS * PARTS)
                        wait(pe, k_moved, (b + 1) * 32)
                    width = GRP * (g + 1)
                    for n, i in enumerate(tiles):
                        q_tile = q_rows[ring][0:K_MAX].rearrange("p h a i -> p (h a i)")[:, i:H * T:NTILE]
                        at = n * width
                        if g:
                            pe.matmul(max_ps[:, k % 2, at:at + width - GRP], q_tile,
                                      k_rows[ring][0:K_MAX, 0:width - GRP], start=True, stop=True)
                        s = pe.matmul(max_ps[:, k % 2, at + width - GRP:at + width], q_tile,
                                      k_mask[ring][0:K_MAX, width - GRP:width], start=True, stop=True)
                    s.then_inc(max_ready, 1)

            def turn(it, ring):
                q, m, b, c = (on(it, s) for s in (has_q, has_m, has_b, has_c))
                rm, rb = (ring - 1) % RING, (ring - 2) % RING
                for slot in range(SLOTS):
                    steps = iter(())
                    if slot < B_LATE and c:
                        steps = scores(it - 3, ring, UNITS - B_LATE + slot)
                    if slot >= B_LATE and b:
                        steps = scores(it - 2, rb, slot - B_LATE)
                    next(steps, None)
                    if m:
                        maxima(it - 1, rm, 4 * slot)
                    next(steps, None)
                    next(steps, None)
                    if m:
                        maxima(it - 1, rm, 4 * slot + 1)
                    if slot == 1 and q:
                        aux_wait(it, "Qk")
                        pe.matmul(aux_ps[0:KQ, :], wdk[:, :, :].rearrange("c g d -> c (g d)"), xnT[:, :],
                                  start=True, stop=True).then_inc(aux_filled, 1)
                    if slot == 2 and q:
                        aux_wait(it, "Qq")
                        pe.matmul(aux_ps[:, :], wdq[:, :], xnT[:, :], start=True, stop=True).then_inc(aux_filled, 1)
                    if slot == 3 and c:
                        turn_products(it, 1, "Yb", it - 3)
                    if slot == 4 and c:
                        aux_wait(it, "Yt")
                        for n in range(NT):
                            s = pe.transpose(aux_ps[:, 128 * n:128 * n + 128], y_t[:, n, :], ident[:, :])
                        s.then_inc(aux_filled, 1)
                    if slot == 5 and c:
                        aux_wait(it, "Cproj")
                        for n in range(NT):
                            s = pe.matmul(aux_ps[:, 128 * n:128 * n + 128], yT[:, 128 * n:128 * n + 128], wp_sb[:, :],
                                          start=True, stop=True)
                        s.then_inc(aux_filled, 1)
                    if slot == 6 and q:
                        aux_wait(it, "Qv")
                        for n in range(NT):
                            s = pe.matmul(aux_ps[:, D * n:D * n + D], xnT[:, 128 * n:128 * n + 128], wdv[:, :],
                                          start=True, stop=True)
                        s.then_inc(aux_filled, 1)
                    if slot == 7 and on(it, has_next):
                        wait(pe, xn_done, (it + 2) * NT)
                        aux_wait(it, "Qtr")
                        for n in range(NT):
                            s = pe.transpose(aux_ps[:, 128 * n:128 * n + 128], xn[:, n, :], ident[:, :])
                        s.then_inc(aux_filled, 1)
                    if slot == 9 and c:
                        wait(pe, xq_done, it - 2)
                        aux_wait(it, "Ctr")
                        for n in range(NT):
                            s = pe.transpose(aux_ps[:, 64 * n:64 * n + 64].bitcast(BF16), xq[:, n, :], ident_b[:, :])
                        s.then_inc(aux_filled, 1)
                    if slot == 10 and c:
                        aux_wait(it, "Cffn")
                        for n in range(NT):
                            s = pe.matmul(aux_ps[:, 128 * n:128 * n + 128], xqT[:, 128 * n:128 * n + 128], wt_T[:, :],
                                          start=True, stop=True)
                        s.then_inc(aux_filled, 1)
                    if slot == 11 and b:
                        turn_products(it, 0, "Ya", it - 2)
                    if m:
                        maxima(it - 1, rm, 4 * slot + 2)
                    if slot <= B_LATE and c:
                        products(it - 3, ring, UNITS - B_LATE - 1 + slot)
                    if slot > B_LATE and b:
                        products(it - 2, rb, slot - B_LATE - 1)
                    if slot == 0 and b:
                        wait(pe, m_split, (it - 1) * 5)
                        aux_wait(it, "Msel")
                        for tl in range(TQ):
                            for n in range(PARTS):
                                s = pe.matmul(aux_ps[0:H * PARTS, NTILE * tl:NTILE * tl + NTILE],
                                              select[:, tl, 32 - H * n:32 - H * n + H * PARTS], m_parts[:, n, :],
                                              start=(n == 0), stop=(n == PARTS - 1))
                        s.then_inc(aux_filled, 1)
                    if m:
                        maxima(it - 1, rm, 4 * slot + 3)

            run_turns(pe, turn)

        @block.scalar
        def _(act):
            act.wait_ge(pe_set, 1)
            act.copy(wdT_sb[:, :], aux_ps[0:LATENT, 0:128]).then_inc(act_set, 1)
            act.wait_ge(pe_set, 2)
            act.copy(wdq[:, :], aux_ps[:, 0:C]).then_inc(act_set, 1)
            for g in range(PARTS * PARTS):
                act.copy(wdk[:, g, :], aux_ps[:, C:C + D]).then_inc(act_set, 1)
            act.copy(wdv[:, :], aux_ps[:, C + D:C + 2 * D]).then_inc(act_set, 1)
            act.wait_ge(pe_set, 3)
            act.copy(wt_T[:, :], pv_ps[:, 0:64].bitcast(BF16)).then_inc(act_set, 1)
            act.wait_ge(part_moved, 32)

            def exps(b, unit):
                hq, kind = divmod(unit, 3)
                for n in range(2 if kind < 2 else 1):
                    chunk = 5 * hq + (0, 2, 4)[kind] + n
                    wait(act, score_ready, b * CHUNKS + (chunk + 1))
                    if n == 0:
                        wait(act, pv_done, b * UNITS + (unit - 2))
                    half = 2 * (chunk % 2)
                    act.activation(probs[kind][:, 1024 * n:1024 * n + 1024],
                                   score_ps[:, half:half + 2].rearrange("p a b -> p (a b)"),
                                   ACT.Exp, scale=SCALE).then_inc(exp_done, 1)

            def copy_products(b, pair):
                wait(act, pv_done, b * UNITS + 6 * (pair + 1))
                act.copy(y_raw[:, pair], pv_ps[:, :]).then_inc(pv_copied, 1)

            def turn(it, ring):
                q, m, b, c = (on(it, s) for s in (has_q, has_m, has_b, has_c))
                for slot in range(SLOTS):
                    if slot == 3 and c:
                        copy_products(it - 3, 1)
                    if slot == 9 and b:
                        copy_products(it - 2, 0)
                    if slot < B_LATE and c:
                        exps(it - 3, UNITS - B_LATE + slot)
                    if slot >= B_LATE and b:
                        exps(it - 2, slot - B_LATE)
                    if slot == 0 and b:
                        wait(act, aux_filled, aux_use(it, "Msel") + 1)
                        wait(act, m_moved, (it - 2) * 16)
                        act.copy(m_rows[:, :], aux_ps[0:H * PARTS, :]).then_inc(aux_free, 1)
                    if slot == 1 and q:
                        wait(act, aux_filled, aux_use(it, "Qk") + 1)
                        act.activation(k1[:, :], aux_ps[0:KQ, :], ACT.Copy, scale=part_col[:, 0:1]).then_inc(k1_done, 1)
                    if slot == 2 and q:
                        wait(act, aux_filled, aux_use(it, "Qq") + 1)
                        wait(act, q_moved, it * 16 * PARTS * PARTS)
                        act.copy(positions(q1), by_position(aux_ps)).then_inc(q1_done, 1)
                    if slot == 4 and c:
                        wait(act, aux_filled, aux_use(it, "Yt") + 1)
                        act.copy(yT[:, :], aux_ps[:, :]).then_inc(aux_free, 1)
                    if slot == 6 and on(it, has_next):
                        if not isinstance(it, int) or it >= 0:
                            wait(act, aux_filled, aux_use(it - 1, "Qtr") + 1)
                        wait(act, ln1_step, (it + 2) * 4)
                        for n in range(NT):
                            act.activation(xn[:, n, :], xa[:, (ring + 1) % RING, n, :], ACT.Identity,
                                           bias=ln1[:, 3, n:n + 1], scale=ln1[:, 2, n:n + 1]).then_inc(xn_done, 1)
                    if slot == 7 and on(it, has_next):
                        wait(act, aux_filled, aux_use(it, "Qtr") + 1)
                        act.copy(xnT[:, :], aux_ps[:, :]).then_inc(aux_free, 1)
                    if slot == 9 and c:
                        wait(act, aux_filled, aux_use(it, "Ctr") + 1)
                        act.copy(xqT[:, :], aux_ps[:, 0:256].bitcast(BF16)).then_inc(aux_free, 1)

            run_turns(act, turn)

        @block.vector
        def _(dve):
            for n in range(RING):
                dve.memset(v_ones[n][:, :, :, :], 0.0).then_inc(dve_set, 1)
            dve.wait_ge(dve_set, RING)
            for n in range(RING):
                for e in range(2):
                    dve.memset(v_ones[n][:, :, e, 16 * e + D:16 * e + 2 * D], 1.0).then_inc(dve_set, 1)
            dve.wait_ge(dve_set, 3 * RING)
            dve.wait_ge(w_loaded, 16 * N_WEIGHTS)
            dve.tensor_scalar(scale_sb[:, 1:2], scale_sb[:, 0:1], EPS, None, ALU.max).then_inc(dve_set, 1)
            dve.wait_ge(dve_set, 3 * RING + 1)
            dve.reciprocal(scale_sb[:, 2:3], scale_sb[:, 1:2]).then_inc(dve_set, 1)
            dve.tensor_scalar(wt_b[:, :], wt_i[:, :], -1.0, None, ALU.add).then_inc(dve_set, 1)
            dve.tensor_scalar(scale_sb[:, 3:4], scale_sb[:, 1:2], BIGGEST, 0.5, ALU.min, ALU.mult).then_inc(dve_set, 1)
            dve.wait_ge(dve_set, 3 * RING + 4)

            def stats(src, st, tiles, signal):
                for n in tiles:
                    dve.bn_stats(st[:, n, :], src[:, n, :]).then_inc(signal, 1)

            def moments(st, mv, b, ready, signal):
                wait(dve, ready, (b + 1) * NT)
                apart(dve, b)
                for n in range(NT):
                    dve.bn_aggr(mv[:, n, :], st[:, n, :]).then_inc(signal, 1)

            def maxima(b, place):
                for k in PLACES[place]:
                    g, tiles = STEPS[k]
                    wait(dve, max_ready, b * NSTEP + (k + 1))
                    if k == 0:
                        wait(dve, m_split, b * 5)
                    n = len(tiles)
                    width = GRP * (g + 1)
                    src = max_ps[:, k % 2, 0:n * width].rearrange("p (n w) -> p n w", n=n)
                    dve.tensor_reduce(neg_max[:, tiles[0]:tiles[0] + n], src, AX_X, ALU.max,
                                      negate=True).then_inc(max_done, 1)

            def invert(it, b, pair, name):
                wait(dve, aux_filled, aux_use(it, name) + 1)
                bank = aux_ps[:, :].rearrange("p (nj k) -> p nj k", k=2 * D)
                dve.reciprocal(y_inv[:, :], bank[:, :, D]).then_inc(inv_done, 1)

            def normalise(b, pair):
                wait(dve, inv_done, b * 2 + (pair + 1))
                bank = aux_ps[:, :].rearrange("p (nj k) -> p nj k", k=2 * D)
                inv = y_inv[:, :].rearrange("p (a b) -> p a b", b=1).broadcast_to([128, NT * H // 2, D])
                half = y_t[:, :, 64 * pair:64 * pair + 64].rearrange("p n (j d) -> p n j d", d=D)
                dve.tensor_tensor(half, bank[:, :, 0:D], inv, ALU.mult).then_inc(aux_free, 1)

            def turn(it, ring):
                q, m, b, c = (on(it, s) for s in (has_q, has_m, has_b, has_c))
                for at in [(slot, place) for slot in range(SLOTS) for place in range(4)]:
                    if at == (0, 0) and b:
                        wait(dve, max_done, (it - 1) * NSTEP)
                        if not isinstance(it, int) or it > 2:
                            wait(dve, aux_filled, aux_use(it - 1, "Msel") + 1)
                        dve.tensor_copy(m_parts[:, 0, :], neg_max[:, :]).then_inc(m_split, 1)
                        wait(dve, m_split, it * 5 - 9)
                        dve.tensor_tensor(m_r[:, 0, :], neg_max[:, :], m_parts[:, 0, :], ALU.subtract).then_inc(m_split, 1)
                        wait(dve, m_split, it * 5 - 8)
                        dve.tensor_copy(m_parts[:, 1, :], m_r[:, 0, :]).then_inc(m_split, 1)
                        wait(dve, m_split, it * 5 - 7)
                        dve.tensor_tensor(m_r[:, 1, :], m_r[:, 0, :], m_parts[:, 1, :], ALU.subtract).then_inc(m_split, 1)
                        wait(dve, m_split, it * 5 - 6)
                        dve.tensor_copy(m_parts[:, 2, :], m_r[:, 1, :]).then_inc(m_split, 1)
                    if m:
                        maxima(it - 1, 4 * at[0] + at[1])
                    if at == (1, 3) and q:
                        wait(dve, k1_done, it + 1)
                        wait(dve, kf_done, it)
                        dve.tensor_tensor(k_r[:, :], aux_ps[0:KQ, :], k1[:, :], ALU.subtract).then_inc(aux_free, 1)
                    if at == (2, 3) and q:
                        wait(dve, q1_done, it + 1)
                        wait(dve, q3_done, it)
                        dve.tensor_tensor(positions(q_r), by_position(aux_ps), positions(q1),
                                          ALU.subtract).then_inc(aux_free, 1)
                    if at == (2, 0) and on(it, has_next):
                        wait(dve, x_loaded, (it + 2) * 16)
                        apart(dve, it)
                        wait(dve, ln1_step, (it + 1) * 4)
                        stats(xa[:, (ring + 1) % RING], st1, range(0, 2), ln1_stats)
                    if at == (2, 1) and on(it, has_next):
                        stats(xa[:, (ring + 1) % RING], st1, range(2, NT), ln1_stats)
                    if at == (3, 0) and on(it, has_next):
                        moments(st1, mv1, it + 1, ln1_stats, ln1_aggr)
                    if at == (3, 2) and c:
                        invert(it, it - 3, 1, "Yb")
                    if at == (3, 3) and c:
                        normalise(it - 3, 1)
                    if at == (11, 2) and b:
                        invert(it, it - 2, 0, "Ya")
                    if at == (11, 3) and b:
                        normalise(it - 2, 0)
                    if at == (5, 2) and c:
                        wait(dve, aux_filled, aux_use(it, "Cproj") + 1)
                        wait(dve, xr_loaded, (it - 2) * 32)
                        dve.tensor_tensor(x1[:, :, :], aux_ps[:, :].rearrange("p (n c) -> p n c", n=NT), xr[:, :, :],
                                          ALU.add).then_inc(aux_free, 1)
                    if at == (5, 3) and c:
                        wait(dve, aux_free, aux_use(it, "Cproj") + 1)
                        apart(dve, it)
                        stats(x1, st2, range(0, 2), ln2_stats)
                    if at == (6, 0) and c:
                        stats(x1, st2, range(2, NT), ln2_stats)
                    if at == (6, 1) and c:
                        moments(st2, mv2, it - 3, ln2_stats, ln2_aggr)
                    if at == (6, 2) and q:
                        wait(dve, aux_filled, aux_use(it, "Qv") + 1)
                        wait(dve, pv_done, (it - 2) * UNITS)
                        v = v_ones[ring][:, :, :, :].rearrange("p n e x -> p n (e x)")
                        for e in range(2):
                            s = dve.tensor_copy(v[:, :, 48 * e:48 * e + D],
                                                aux_ps[:, 0:NT * D].rearrange("p (n d) -> p n d", n=NT))
                        s.then_inc(aux_free, 1)
                    if at == (8, 3) and c:
                        wait(dve, zb_done, it - 2)
                        dve.tensor_scalar(z_lo[:, :, :], zb[:, :, :], QB, -QB, ALU.min, ALU.max).then_inc(clipped, 1)
                        dve.tensor_scalar(z_hi[:, :, :], zb[:, :, :], -QB, QB, ALU.max, ALU.min).then_inc(clipped, 1)
                    if at == (9, 0) and c:
                        wait(dve, clipped, (it - 2) * 2)
                        dve.tensor_tensor(xq[:, :, :], z_lo[:, :, :], z_hi[:, :, :], ALU.add).then_inc(xq_done, 1)
                    if at == (10, 3) and c:
                        wait(dve, aux_filled, aux_use(it, "Cffn") + 1)
                        wait(dve, x1b_done, it - 2)
                        wait(dve, o_stored, (it - 2) * 32)
                        dve.scalar_tensor_tensor(out=o_sb[:, :, :].rearrange("p n c -> p (n c)"), in0=aux_ps[:, :],
                                                 scalar=scale_sb[:, 3:4],
                                                 in1=x1b[:, :, :].rearrange("p n c -> p (n c)"),
                                                 op0=ALU.mult, op1=ALU.add).then_inc(aux_free, 1)

            run_turns(dve, turn)

        @block.gpsimd
        def _(pool):
            count = [0]

            def done(ins):
                ins.then_inc(pool_set, 1)
                count[0] += 1
                pool.wait_ge(pool_set, count[0])

            def keep(tile, compare, fill, base, pattern, channel):
                done(pool.affine_select(out=tile, in_=tile, compare_op=compare, fill=fill, base=base,
                                        pattern=pattern, channel_multiplier=channel))

            for square in (ident, ident_b):
                done(pool.memset(square[:, :], 0.0))
                keep(square[:, :], ALU.not_equal, 1.0, 0, [[-1, 128]], 1)
            done(pool.memset(half_neg[:, :], -0.5))
            done(pool.memset(part_row[:, :, :, :, :], 0.0))
            done(pool.memset(part_row[:, 0, :, 1:3, :], 1.0))
            done(pool.memset(part_row[:, 1, :, 2:3, :], 1.0))
            done(pool.memset(one_hot[:, :, :], 0.0))
            hot = one_hot[64:96].rearrange("p a (g b) -> p a g b", b=GRP // TQ)
            keep(hot, ALU.not_equal, 1.0, R_MASK - 64, [[1, TQ], [0, T // GRP], [TQ, GRP // TQ]], -1)
            assert count[0] == HOT_SET
            done(pool.memset(select[:, :, :], 0.0))
            keep(select[:, :, :], ALU.not_equal, 1.0, TQ * 32, [[-1, TQ], [-TQ, 80]], 1)
            for n in range(RING):
                done(pool.memset(k_rows[n][64:96, :], 0.0))
                done(pool.memset(k_rows[n][96:128, :], 1.0))
                done(pool.memset(k_mask[n][64:96, :], 0.0))
                keep(k_mask[n][64:96, :].rearrange("p (g t) -> p g t", t=GRP), ALU.is_ge, NEG, -(R_MASK - 64),
                     [[0, T // GRP], [-1, GRP]], 1)
            assert count[0] == POOL_SET

            def small_ln(mv, ln, step, b, per, aggr):
                wait(pool, aggr, (b + 1) * NT)
                apart(pool, b)
                pool.tensor_scalar(ln[:, 0, :], mv[:, :, 1], EPS, 1.0, ALU.add, ALU.mult).then_inc(step, 1)
                pool.tensor_scalar(ln[:, 1, :], mv[:, :, 0], -1.0, 0.0, ALU.mult, ALU.add).then_inc(step, 1)
                wait(pool, step, b * per + 2)
                pool.tensor_tensor(ln[:, 2, :], ln[:, 0, :], half_neg[:, :], ALU.pow).then_inc(step, 1)
                wait(pool, step, b * per + 3)

            def small_ln1(b):
                wait(pool, xn_done, b * NT)
                small_ln(mv1, ln1, ln1_step, b, 4, ln1_aggr)
                pool.tensor_tensor(ln1[:, 3, :], ln1[:, 1, :], ln1[:, 2, :], ALU.mult).then_inc(ln1_step, 1)

            def select_causal(b, unit):
                hq, kind = divmod(unit, 3)
                wait(pool, exp_done, b * CHUNKS + (5 * hq + (2, 4, 5)[kind]))
                apart(pool, b)
                tiles = probs[kind][:, :].rearrange("p (ra i) -> p ra i", i=32 if kind == 2 else 64)
                for at in {0: [0], 1: [0, 48], 2: [0]}[kind]:
                    v = tiles[:, :, at:at + 16]
                    pool.affine_select(out=v, in_=v, compare_op=ALU.is_ge, fill=0.0, base=0,
                                       pattern=[[0, 4], [1, TQ], [TQ, 16]],
                                       channel_multiplier=-1).then_inc(masked, 1)

            def normalise2(b):
                small_ln(mv2, ln2, ln2_step, b, 5, ln2_aggr)
                apart(pool, b)
                pool.tensor_scalar(ln2[:, 4, :], ln2[:, 2, :], scale_sb[:, 2:3], 0.0, ALU.mult, ALU.add).then_inc(ln2_step, 1)
                wait(pool, ln2_step, b * 5 + 4)
                pool.tensor_tensor(ln2[:, 3, :], ln2[:, 1, :], ln2[:, 4, :], ALU.mult).then_inc(ln2_step, 1)
                wait(pool, ln2_step, (b + 1) * 5)
                apart(pool, b)
                for n in range(NT):
                    pool.tensor_scalar(z[:, n, :], x1[:, n, :], ln2[:, 4, n:n + 1], ln2[:, 3, n:n + 1],
                                       ALU.mult, ALU.add).then_inc(z_step, 1)

            def round_z(b):
                wait(pool, z_step, b * (NT + 1) + NT)
                apart(pool, b)
                pool.tensor_scalar(z_up[:, :, :], z[:, :, :], 1.0, ROUND, ALU.mult, ALU.add).then_inc(z_step, 1)
                wait(pool, z_step, (b + 1) * (NT + 1))
                apart(pool, b)
                pool.tensor_scalar(zb[:, :, :], z_up[:, :, :], -ROUND, 1.0, ALU.add, ALU.mult).then_inc(zb_done, 1)

            pool.wait_ge(w_loaded, 16 * N_WEIGHTS)
            pool.wait_ge(part_moved, 32)
            pool.wait_ge(dve_set, 3 * RING + 4)

            def turn(it, ring):
                q, m, b, c = (on(it, s) for s in (has_q, has_m, has_b, has_c))
                for slot in range(SLOTS):
                    if slot < B_LATE and c:
                        select_causal(it - 3, UNITS - B_LATE + slot)
                    if slot >= B_LATE and b:
                        select_causal(it - 2, slot - B_LATE)
                    if slot == 2 and q:
                        wait(pool, aux_free, aux_use(it, "Qk") + 1)
                        wait(pool, k_moved, it * 32)
                        apart(pool, it)
                        pool.tensor_scalar(k2[:, :], k_r[:, :], part_col[:, 1:2], 0.0, ALU.mult, ALU.add).then_inc(k2_done, 1)
                        wait(pool, k2_done, it + 1)
                        pool.tensor_tensor(kf[:, :], k_r[:, :], k2[:, :], ALU.subtract).then_inc(kf_done, 1)
                    if slot == 3 and q:
                        wait(pool, aux_free, aux_use(it, "Qq") + 1)
                        wait(pool, q_moved, it * 16 * PARTS * PARTS)
                        apart(pool, it)
                        pool.tensor_scalar(q2[:, :], q_r[:, :], 1.0, 0.0, ALU.mult, ALU.add).then_inc(q2_done, 1)
                        wait(pool, q2_done, it + 1)
                        pool.tensor_tensor(q3[:, :], q_r[:, :], q2[:, :], ALU.subtract).then_inc(q3_done, 1)
                    if slot == 4 and on(it, has_next):
                        small_ln1(it + 1)
                    if slot == 6 and c:
                        normalise2(it - 3)
                    if slot == 7 and c:
                        if not isinstance(it, int) or it > 3:
                            wait(pool, aux_free, aux_use(it - 1, "Cffn") + 1)
                        round_z(it - 3)
                    if slot == 8 and c:
                        pool.tensor_tensor(x1b[:, :, :], x1[:, :, :],
                                           bias_sb[:, :].rearrange("p (a c) -> p a c", a=1).broadcast_to([128, NT, C]),
                                           ALU.add).then_inc(x1b_done, 1)

            run_turns(pool, turn)


_INS = ["L0_attn_x", "L0_attn_Wc_down", "L0_attn_Wq_up", "L0_attn_Wkv_up", "L0_attn_Wc_proj",
        "L0_ffn_ternary_weight", "L0_ffn_bias", "L0_ffn_act_scale"]


def kernel(**inputs):
    import numpy as _np
    import concourse.bacc as _bacc
    from concourse import mybir as _mybir
    from concourse.bass_utils import run_bass_kernel_spmd as _run

    nc = _bacc.Bacc("TRN2", target_bir_lowering=False, num_devices=1)
    arrays, args = {}, []
    for name in _INS:
        a = _np.ascontiguousarray(inputs[name])
        if name == "L0_ffn_act_scale":
            a = a.reshape(1, 1)
        arrays[f"in_{name}_dram"] = a
        args.append(nc.dram_tensor(f"in_{name}_dram", a.shape, _mybir.dt.from_np(a.dtype), kind="ExternalInput").ap())
    args.append(nc.dram_tensor("out_dram", (NB, T, C), _mybir.dt.float32, kind="ExternalOutput").ap())
    program(nc, *args)
    r = _run(nc, [arrays], core_ids=[0])
    return r.results[0]["out_dram"]
```

```python
from contextlib import ExitStack

import concourse.bass as bass
from concourse import mybir

F32 = mybir.dt.float32
BF16 = mybir.dt.bfloat16
I32 = mybir.dt.int32
ALU = mybir.AluOpType
ACT = mybir.ActivationFunctionType
AX_X = mybir.AxisListType.X

NB, T, C = 16, 512, 128
H, D = 16, 8
LATENT = 64
NT = T // 128
PARTS = 3
KQ = PARTS * PARTS * D
KV = KQ + D
GRP = 16
R_MASK = KQ
K_MAX = 96
R_M = 96
K_S = R_M + PARTS
TQ = 8
NTILE = T // TQ
NEG = -1.0e38
SCALE = 1.0 / float(D) ** 0.5
EPS = 1e-5
QB = 127.0
ROUND = 12582912.0
BIGGEST = 3.0e38
RING = 3

HQ = 4
MASKS = 16
CHUNKS = 40
UNITS = 12
SLOTS = UNITS
MAX_FROM, MAX_TO = 2, 46
B_LATE = 2
PV_LATE = B_LATE + 2
STEPS = [(g, (2 * g, 2 * g + 1)) for g in range(16)] + [(i // 2, (i,)) for i in range(32, NTILE)]
NSTEP = len(STEPS)


def step_places():
    share = []
    for slot in range(SLOTS):
        other = (1 if (slot - B_LATE) % 3 == 2 else 2) + (1 if (slot - PV_LATE) % 3 == 2 else 2)
        other += 2 if slot < 9 else 0.5
        share += [1 + 0.2 * (5 - other)] * 4
    share = share[MAX_FROM:MAX_TO]
    cost = [len(tiles) * GRP * (g + 1) + 100 for g, tiles in STEPS]
    out = [[] for _ in range(4 * SLOTS)]
    place, filled, at = 0, share[0], 0
    for k, c in enumerate(cost):
        middle = (at + c / 2) / sum(cost) * sum(share)
        while middle > filled and place + 1 < len(share):
            place += 1
            filled += share[place]
        out[MAX_FROM + place].append(k)
        at += c
    return out


PLACES = step_places()

def has_q(it): return 0 <= it < NB
def has_m(it): return 0 <= it - 1 < NB
def has_b(it): return 0 <= it - 2 < NB
def has_c(it): return 0 <= it - 3 < NB
def has_next(it): return 0 <= it + 1 < NB

FIRST_TURN, LAST_TURN = -1, NB + 3
STEADY = (3, NB - 1)
AUX = [("Msel", has_b), ("Qk", has_q), ("Qq", has_q), ("Ya", has_c), ("Yb", has_c), ("Yt", has_c),
       ("Cproj", has_c), ("Qv", has_q), ("Qtr", has_next), ("Ctr", has_c), ("Cffn", has_c)]


def aux_use(it, name):
    if isinstance(it, int):
        before = sum(on(e) for e in range(FIRST_TURN, it) for _, on in AUX)
        for n, on in AUX:
            if n == name:
                return before
            before += on(it)
    start = sum(on(e) for e in range(FIRST_TURN, STEADY[0]) for _, on in AUX)
    return (it - STEADY[0]) * len(AUX) + (start + [n for n, _ in AUX].index(name))


def head_of(hq, r):
    return 8 * (hq // 2) + 2 * r + hq % 2


def wait(eng, sem, value):
    if not isinstance(value, int) or value > 0:
        eng.wait_ge(sem, value)


def program(nc, x, w_down, w_q, w_kv, w_proj, w_tern, bias, act_scale, out):
    with ExitStack() as ctx:
        def sb(name, shape, dt):
            return ctx.enter_context(nc.sbuf_tensor(name, shape, dt))

        def sem(name):
            return ctx.enter_context(nc.semaphore(name))

        score_ps = ctx.enter_context(nc.psum_tensor("score_ps", [128, 3, 512], F32))
        pv_ps = ctx.enter_context(nc.psum_tensor("pv_ps", [128, 512], F32))
        max_ps = ctx.enter_context(nc.psum_tensor("max_ps", [128, 3, 512], F32))
        aux_ps = ctx.enter_context(nc.psum_tensor("aux_ps", [128, 512], F32))

        ident = sb("ident", [128, 128], F32)
        ident_b = sb("ident_b", [128, 128], BF16)
        select = sb("select", [128, TQ, 80], BF16)
        half_neg = sb("half_neg", [128, NT], F32)
        part_row = sb("part_row", [1, 2, PARTS * PARTS + 1, D], F32)
        part_col = sb("part_col", [KV, 2], F32)
        wd_sb = sb("wd_sb", [128, LATENT], F32)
        wdT_sb = sb("wdT_sb", [LATENT, 128], F32)
        wq_sb = sb("wq_sb", [LATENT, C], F32)
        wkv_sb = sb("wkv_sb", [LATENT, 2 * D], F32)
        wdq = sb("wdq", [128, C], F32)
        wdkv = sb("wdkv", [128, PARTS * PARTS + 1, D], F32)
        wp_sb = sb("wp_sb", [128, C], F32)
        wt_i = sb("wt_i", [128, C], I32)
        wt_b = sb("wt_b", [128, C], BF16)
        wt_T = sb("wt_T", [128, C], BF16)
        bias_sb = sb("bias_sb", [128, C], F32)
        scale_sb = sb("scale_sb", [128, 4], F32)

        xa = sb("xa", [128, RING, NT, C], F32)
        st1 = sb("st1", [128, NT, 6], F32)
        mv1 = sb("mv1", [128, NT, 2], F32)
        ln1 = sb("ln1", [128, 4, NT], F32)
        xn = sb("xn", [128, NT, C], F32)
        xnT = sb("xnT", [128, T], F32)
        q1 = sb("q1", [128, T], BF16)
        q_r = sb("q_r", [128, T], F32)
        q2 = sb("q2", [128, T], BF16)
        q3 = sb("q3", [128, T], BF16)
        k1 = sb("k1", [KV, T], BF16)
        k_r = sb("k_r", [KV, T], F32)
        k2 = sb("k2", [KQ, T], BF16)
        kf = sb("kf", [KQ, T], BF16)
        one_hot = sb("one_hot", [128, TQ, NTILE], BF16)
        q_rows = [sb(f"q_rows{n}", [128, H, TQ, NTILE], BF16) for n in range(RING)]
        k_rows = [sb(f"k_rows{n}", [128, T], BF16) for n in range(RING)]
        k_mask = [sb(f"k_mask{n}", [128, T], BF16) for n in range(RING)]
        v_ones = [sb(f"v_ones{n}", [128, NT, 2, 32], F32) for n in range(RING)]
        neg_max = sb("neg_max", [128, NTILE], F32)
        m_r = sb("m_r", [128, 2, NTILE], F32)
        m_parts = sb("m_parts", [128, PARTS, NTILE], BF16)
        m_rows = sb("m_rows", [H * PARTS, T], BF16)
        probs = [sb(f"probs{n}", [128, w], F32) for n, w in enumerate((2048, 2048, 1024))]
        y_raw = sb("y_raw", [128, 2, T], F32)
        y_inv = sb("y_inv", [128, NT * H // 2], F32)
        y_t = sb("y_t", [128, NT, C], F32)
        yT = sb("yT", [128, T], F32)
        xr = sb("xr", [128, NT, C], F32)
        x1 = sb("x1", [128, NT, C], F32)
        x1b = sb("x1b", [128, NT, C], F32)
        st2 = sb("st2", [128, NT, 6], F32)
        mv2 = sb("mv2", [128, NT, 2], F32)
        ln2 = sb("ln2", [128, 5, NT], F32)
        z = sb("z", [128, NT, C], F32)
        z_up = sb("z_up", [128, NT, C], F32)
        zb = sb("zb", [128, NT, C], BF16)
        z_lo = sb("z_lo", [128, NT, C], BF16)
        z_hi = sb("z_hi", [128, NT, C], BF16)
        xq = sb("xq", [128, NT, C], BF16)
        xqT = sb("xqT", [128, T], BF16)
        o_sb = sb("o_sb", [128, NT, C], F32)

        qkv_loaded = sem("qkv_loaded")
        w_loaded = sem("w_loaded")
        pool_set = sem("pool_set")
        dve_set = sem("dve_set")
        act_set = sem("act_set")
        pe_set = sem("pe_set")
        part_moved = sem("part_moved")
        hot_moved = sem("hot_moved")
        x_loaded = sem("x_loaded")
        ln1_stats = sem("ln1_stats")
        ln1_aggr = sem("ln1_aggr")
        ln1_step = sem("ln1_step")
        xn_done = sem("xn_done")
        aux_filled = sem("aux_filled")
        aux_free = sem("aux_free")
        q1_done = sem("q1_done")
        q2_done = sem("q2_done")
        q3_done = sem("q3_done")
        k1_done = sem("k1_done")
        k2_done = sem("k2_done")
        kf_done = sem("kf_done")
        q_moved = sem("q_moved")
        k_moved = sem("k_moved")
        max_ready = sem("max_ready")
        max_done = sem("max_done")
        m_split = sem("m_split")
        m_moved = sem("m_moved")
        score_ready = sem("score_ready")
        exp_done = sem("exp_done")
        masked = sem("masked")
        pv_done = sem("pv_done")
        pv_copied = sem("pv_copied")
        inv_done = sem("inv_done")
        xr_loaded = sem("xr_loaded")
        ln2_stats = sem("ln2_stats")
        ln2_aggr = sem("ln2_aggr")
        ln2_step = sem("ln2_step")
        z_step = sem("z_step")
        zb_done = sem("zb_done")
        clipped = sem("clipped")
        xq_done = sem("xq_done")
        x1b_done = sem("x1b_done")
        o_stored = sem("o_stored")

        carried = sem("carried")

        N_QKV, N_WEIGHTS = 3, 4
        PART_SET = 8
        HOT_SET = PART_SET + 2
        POOL_SET = HOT_SET + 2 + 4 * RING

        def tokens(dram):
            return dram.rearrange("(n p) c -> p n c", p=128)

        def halves(dram):
            v = dram.rearrange("(i n a) c -> a i n c", n=NT, a=2)
            return v[0], v[1]

        def apart(eng, value):
            if not isinstance(value, int):
                eng.sem_inc(carried, 1)

        def positions(a):
            return a[:, :].rearrange("p (a i) -> p a i", a=TQ)

        def by_position(a):
            return a[:, :].rearrange("p (i a) -> p a i", a=TQ)

        def run_turns(eng, turn):
            for it in range(FIRST_TURN, STEADY[0]):
                turn(it, it % RING)
            with eng.Fori(0, (STEADY[1] - STEADY[0]) // RING) as i:
                for u in range(RING):
                    turn(i * RING + (STEADY[0] + u), (STEADY[0] + u) % RING)
            for it in range(STEADY[1], LAST_TURN):
                turn(it, it % RING)

        def on(it, stage):
            return stage(it) if isinstance(it, int) else True

        block = ctx.enter_context(nc.Block())

        @block.sync
        def _(sp):
            def turn(it, ring):
                if on(it, has_next):
                    wait(sp, xn_done, (it + 1) * NT)
                    sp.dma_start(xa[:, (ring + 1) % RING], tokens(x[it + 1])).then_inc(x_loaded, 16)
                if on(it, has_b):
                    wait(sp, aux_free, aux_use(it, "Msel") + 1)
                    sp.dma_start(q_rows[(ring - 2) % RING][R_M:R_M + PARTS], m_rows[:, :]).then_inc(m_moved, 16)
                if on(it, has_c):
                    if not isinstance(it, int) or it > 3:
                        wait(sp, aux_free, aux_use(it - 1, "Cproj") + 1)
                    for n, half in enumerate(halves(x[it - 3])):
                        sp.dma_start(xr[64 * n:64 * n + 64], half).then_inc(xr_loaded, 16)
                if on(it, has_q):
                    if isinstance(it, int) and it == 0:
                        sp.wait_ge(pool_set, HOT_SET)
                        for n in range(RING):
                            sp.dma_start(q_rows[n][64:96].rearrange("p h a i -> p h (a i)"),
                                         one_hot[64:96].rearrange("p (h a) i -> p h (a i)", h=1).broadcast_to([32, H, T])).then_inc(hot_moved, 16)
                        sp.wait_ge(pool_set, POOL_SET)
                        sp.wait_ge(hot_moved, 16 * RING)
                    wait(sp, score_ready, (it - 2) * CHUNKS)

                    def move_queries(part, a, done):
                        wait(sp, done, it + 1)
                        for g in range(PARTS):
                            row = (a * PARTS + g) * D
                            sp.dma_start(q_rows[ring][row:row + D], part[:, :]).then_inc(q_moved, 16)

                    move_queries(q1, 0, q1_done)
                    wait(sp, kf_done, it + 1)
                    sp.dma_start(k_rows[ring][0:KQ, :], kf[:, :]).then_inc(k_moved, 16)
                    wait(sp, max_ready, (it - 2) * NSTEP)
                    sp.dma_start(k_mask[ring][0:KQ, :], kf[:, :]).then_inc(k_moved, 16)
                    move_queries(q2, 1, q2_done)
                    move_queries(q3, 2, q3_done)
                if on(it, has_c):
                    wait(sp, aux_free, aux_use(it, "Cffn") + 1)
                    for n, half in enumerate(halves(out[it - 3])):
                        sp.dma_start(half, o_sb[64 * n:64 * n + 64]).then_inc(o_stored, 16)

            sp.sem_inc(o_stored, 32)
            run_turns(sp, turn)
            sp.wait_ge(o_stored, 32 * (NB + 1))

        @block.tensor
        def _(pe):
            pe.wait_ge(qkv_loaded, 16 * N_QKV)
            pe.wait_ge(pool_set, 4)
            pe.transpose(aux_ps[0:LATENT, 0:128], wd_sb[:, :], ident[:, :]).then_inc(pe_set, 1)
            pe.wait_ge(act_set, 1)
            pe.matmul(aux_ps[:, 0:C], wdT_sb[:, :], wq_sb[:, :].rearrange("l (h d) -> l d h", d=D),
                      start=True, stop=True)
            pe.matmul(aux_ps[:, C:C + 2 * D], wdT_sb[:, :], wkv_sb[:, :], start=True, stop=True).then_inc(pe_set, 1)
            pe.wait_ge(act_set, 2 + PARTS * PARTS + 1)

            def aux_wait(it, name):
                wait(pe, aux_free, aux_use(it, name))

            def scores(b, ring, unit):
                hq, kind = divmod(unit, 3)
                kr = k_rows[ring]

                def queries(head, j):
                    return q_rows[ring][0:K_S, head, :, 16 * j:NTILE]

                for n in range(4 if kind < 2 else 2):
                    chunk = 10 * hq + 4 * kind + n
                    wait(pe, exp_done, b * CHUNKS + (chunk - 2))
                    if unit == 0 and n == 0:
                        wait(pe, m_moved, (b + 1) * 16)
                    bank = score_ps[:, (ring + chunk) % 3]
                    if kind == 0:
                        s = pe.matmul(bank, kr[0:K_S, 0:128], queries(head_of(hq, n), 0), start=True, stop=True)
                    elif kind == 1:
                        bank = bank.rearrange("p (a i) -> p a i", a=TQ)
                        pe.matmul(bank[:, :, 0:48], kr[0:K_S, 128:256], queries(head_of(hq, n), 1),
                                  start=True, stop=True)
                        s = pe.matmul(bank[:, :, 48:64], kr[0:K_S, 384:512], queries(head_of(hq, n), 3),
                                      start=True, stop=True)
                    else:
                        for e in range(2):
                            s = pe.matmul(bank[:, 256 * e:256 * e + 256], kr[0:K_S, 256:384],
                                          queries(head_of(hq, 2 * n + e), 2), start=True, stop=True)
                    s.then_inc(score_ready, 1)
                    yield

            def products(b, ring, unit):
                hq, kind = divmod(unit, 3)
                wait(pe, masked, b * MASKS + (4 * hq + (1, 3, 4)[kind]))
                if kind == 0 and hq % 2 == 0:
                    wait(pe, pv_copied, b * 2 + hq // 2)
                v, p = v_ones[ring], probs[kind][:, :]
                pieces = {0: [(0, 0, 64)], 1: [(1, 0, 64), (3, 48, 64)], 2: [(2, 0, 32)]}[kind]
                for j, at, pitch in pieces:
                    heads = p.rearrange("p (r a i) -> p r a i", r=4, i=pitch)
                    for r in range(4):
                        rows = pv_ps[32 * r:32 * r + 32, :].rearrange("p (a i) -> p a i", a=TQ)
                        s = pe.matmul(rows[:, :, 16 * j:NTILE], v[:, j, hq % 2, :],
                                      heads[:, r, :, at:at + NTILE - 16 * j],
                                      start=(kind == 0 and hq % 2 == 0), stop=(kind == 2 and hq % 2 == 1), skip_group_check=True)
                s.then_inc(pv_done, 1)

            def turn_products(it, pair, name, b):
                wait(pe, pv_copied, b * 2 + (pair + 1))
                aux_wait(it, name)
                for n in range(NT):
                    s = pe.transpose(aux_ps[:, 128 * n:128 * n + 128], y_raw[:, pair, 128 * n:128 * n + 128], ident[:, :])
                s.then_inc(aux_filled, 1)

            def maxima(b, ring, place):
                for k in PLACES[place]:
                    g, tiles = STEPS[k]
                    wait(pe, max_done, b * NSTEP + (k - 2))
                    if k == 0:
                        wait(pe, q_moved, (b + 1) * 16 * PARTS * PARTS)
                        wait(pe, k_moved, (b + 1) * 32)
                    width = GRP * (g + 1)
                    for n, i in enumerate(tiles):
                        q_tile = q_rows[ring][0:K_MAX].rearrange("p h a i -> p (h a i)")[:, i:H * T:NTILE]
                        at = n * width
                        if g:
                            pe.matmul(max_ps[:, k % 3, at:at + width - GRP], q_tile,
                                      k_rows[ring][0:K_MAX, 0:width - GRP], start=True, stop=True)
                        s = pe.matmul(max_ps[:, k % 3, at + width - GRP:at + width], q_tile,
                                      k_mask[ring][0:K_MAX, width - GRP:width], start=True, stop=True)
                    s.then_inc(max_ready, 1)

            def turn(it, ring):
                q, m, b, c = (on(it, s) for s in (has_q, has_m, has_b, has_c))
                rm, rb = (ring - 1) % RING, (ring - 2) % RING
                for slot in range(SLOTS):
                    steps = iter(())
                    if slot < B_LATE and c:
                        steps = scores(it - 3, ring, UNITS - B_LATE + slot)
                    if slot >= B_LATE and b:
                        steps = scores(it - 2, rb, slot - B_LATE)
                    next(steps, None)
                    next(steps, None)
                    if m:
                        maxima(it - 1, rm, 4 * slot)
                    if slot < PV_LATE and c:
                        products(it - 3, ring, UNITS - PV_LATE + slot)
                    if slot >= PV_LATE and b:
                        products(it - 2, rb, slot - PV_LATE)
                    if m:
                        maxima(it - 1, rm, 4 * slot + 1)
                    next(steps, None)
                    if m:
                        maxima(it - 1, rm, 4 * slot + 2)
                    next(steps, None)
                    if slot == 1 and q:
                        aux_wait(it, "Qk")
                        pe.matmul(aux_ps[0:KV, :], wdkv[:, :, :].rearrange("c g d -> c (g d)"), xnT[:, :],
                                  start=True, stop=True).then_inc(aux_filled, 1)
                    if slot == 2 and q:
                        aux_wait(it, "Qq")
                        pe.matmul(aux_ps[:, :], wdq[:, :], xnT[:, :], start=True, stop=True).then_inc(aux_filled, 1)
                    if slot == 3 and c:
                        turn_products(it, 0, "Ya", it - 3)
                    if slot == 4 and c:
                        turn_products(it, 1, "Yb", it - 3)
                    if slot == 5 and c:
                        aux_wait(it, "Yt")
                        for n in range(NT):
                            s = pe.transpose(aux_ps[:, 128 * n:128 * n + 128], y_t[:, n, :], ident[:, :])
                        s.then_inc(aux_filled, 1)
                    if slot == 6 and c:
                        aux_wait(it, "Cproj")
                        for n in range(NT):
                            s = pe.matmul(aux_ps[:, 128 * n:128 * n + 128], yT[:, 128 * n:128 * n + 128], wp_sb[:, :],
                                          start=True, stop=True)
                        s.then_inc(aux_filled, 1)
                    if slot == 7 and q:
                        aux_wait(it, "Qv")
                        for n in range(NT):
                            s = pe.matmul(aux_ps[:, 16 * n:16 * n + 16], k_r[64:KV, 128 * n:128 * n + 128],
                                          ident[64:KV, 64:KV], start=True, stop=True)
                        s.then_inc(aux_filled, 1)
                    if slot == 8 and on(it, has_next):
                        wait(pe, xn_done, (it + 2) * NT)
                        aux_wait(it, "Qtr")
                        for n in range(NT):
                            s = pe.transpose(aux_ps[:, 128 * n:128 * n + 128], xn[:, n, :], ident[:, :])
                        s.then_inc(aux_filled, 1)
                    if slot == 9 and isinstance(it, int) and it == 0:
                        pe.wait_ge(dve_set, 3 * RING + 3)
                        pe.transpose(pv_ps[:, 0:64].bitcast(BF16), wt_b[:, :], ident_b[:, :]).then_inc(pe_set, 1)
                    if slot == 0 and isinstance(it, int) and it == 1:
                        pe.wait_ge(w_loaded, 16 * N_WEIGHTS)
                        pe.wait_ge(act_set, 2 + PARTS * PARTS + 2)
                    if slot == 11 and c:
                        aux_wait(it, "Cffn")
                        for n in range(NT):
                            s = pe.matmul(aux_ps[:, 128 * n:128 * n + 128], xqT[:, 128 * n:128 * n + 128], wt_T[:, :],
                                          start=True, stop=True)
                        s.then_inc(aux_filled, 1)
                    if slot == 10 and c:
                        wait(pe, xq_done, it - 2)
                        aux_wait(it, "Ctr")
                        for n in range(NT):
                            s = pe.transpose(aux_ps[:, 64 * n:64 * n + 64].bitcast(BF16), xq[:, n, :], ident_b[:, :])
                        s.then_inc(aux_filled, 1)
                    if slot == 0 and b:
                        wait(pe, m_split, (it - 1) * 5)
                        aux_wait(it, "Msel")
                        for tl in range(TQ):
                            for n in range(PARTS):
                                s = pe.matmul(aux_ps[0:H * PARTS, NTILE * tl:NTILE * tl + NTILE],
                                              select[:, tl, 32 - H * n:32 - H * n + H * PARTS], m_parts[:, n, :],
                                              start=(n == 0), stop=(n == PARTS - 1))
                        s.then_inc(aux_filled, 1)
                    if m:
                        maxima(it - 1, rm, 4 * slot + 3)

            run_turns(pe, turn)

        @block.scalar
        def _(act):
            act.dma_start(wd_sb[:, :], w_down).then_inc(qkv_loaded, 16)
            act.dma_start(wq_sb[:, :], w_q).then_inc(qkv_loaded, 16)
            act.dma_start(wkv_sb[:, :], w_kv).then_inc(qkv_loaded, 16)
            act.dma_start(wt_i[:, :], w_tern).then_inc(w_loaded, 16)
            act.dma_start(bias_sb[:, :], bias.rearrange("(a c) -> a c", a=1).broadcast_to([128, C])).then_inc(w_loaded, 16)
            act.dma_start(scale_sb[:, 0:1], act_scale.broadcast_to([128, 1])).then_inc(w_loaded, 16)
            act.dma_start(wp_sb[:, :], w_proj).then_inc(w_loaded, 16)
            act.wait_ge(pe_set, 1)
            act.copy(wdT_sb[:, :], aux_ps[0:LATENT, 0:128]).then_inc(act_set, 1)
            act.wait_ge(pe_set, 2)
            act.copy(wdq[:, :], aux_ps[:, 0:C]).then_inc(act_set, 1)
            for g in range(PARTS * PARTS):
                act.copy(wdkv[:, g, :], aux_ps[:, C:C + D]).then_inc(act_set, 1)
            act.copy(wdkv[:, PARTS * PARTS, :], aux_ps[:, C + D:C + 2 * D]).then_inc(act_set, 1)
            act.wait_ge(pool_set, PART_SET)
            for n in range(2):
                act.dma_start(part_col[:, n:n + 1], part_row[0:1, n].rearrange("a g d -> a (g d)")).then_inc(part_moved, 16)

            def exps(b, ring, unit):
                hq, kind = divmod(unit, 3)
                for n in range(4 if kind < 2 else 2):
                    chunk = 10 * hq + 4 * kind + n
                    wait(act, score_ready, b * CHUNKS + (chunk + 1))
                    if n == 0:
                        wait(act, pv_done, b * UNITS + (unit - 2))
                    act.activation(probs[kind][:, 512 * n:512 * n + 512], score_ps[:, (ring + chunk) % 3],
                                   ACT.Exp, scale=SCALE).then_inc(exp_done, 1)

            def copy_products(b, pair):
                wait(act, pv_done, b * UNITS + 6 * (pair + 1))
                act.copy(y_raw[:, pair], pv_ps[:, :]).then_inc(pv_copied, 1)

            def turn(it, ring):
                q, m, b, c = (on(it, s) for s in (has_q, has_m, has_b, has_c))
                for slot in range(SLOTS):
                    if slot == PV_LATE and c:
                        copy_products(it - 3, 1)
                    if slot == PV_LATE + 6 and b:
                        copy_products(it - 2, 0)
                    if slot < B_LATE and c:
                        exps(it - 3, ring, UNITS - B_LATE + slot)
                    if slot >= B_LATE and b:
                        exps(it - 2, (ring - 2) % RING, slot - B_LATE)
                    if slot == 0 and b:
                        wait(act, aux_filled, aux_use(it, "Msel") + 1)
                        wait(act, m_moved, (it - 2) * 16)
                        act.copy(m_rows[:, :], aux_ps[0:H * PARTS, :]).then_inc(aux_free, 1)
                    if slot == 1 and q:
                        if isinstance(it, int) and it == 0:
                            act.wait_ge(part_moved, 32)
                        wait(act, aux_filled, aux_use(it, "Qk") + 1)
                        act.activation(k1[:, :], aux_ps[0:KV, :], ACT.Copy, scale=part_col[:, 0:1]).then_inc(k1_done, 1)
                    if slot == 2 and q:
                        wait(act, aux_filled, aux_use(it, "Qq") + 1)
                        wait(act, q_moved, it * 16 * PARTS * PARTS)
                        act.copy(positions(q1), by_position(aux_ps)).then_inc(q1_done, 1)
                    if slot == 5 and c:
                        wait(act, aux_filled, aux_use(it, "Yt") + 1)
                        act.copy(yT[:, :], aux_ps[:, :]).then_inc(aux_free, 1)
                    if slot in (6, 7) and on(it, has_next):
                        if not isinstance(it, int) or it >= 0:
                            wait(act, aux_filled, aux_use(it - 1, "Qtr") + 1)
                        wait(act, ln1_step, (it + 2) * 4)
                        for n in ((0, 1), (2, 3))[slot - 6]:
                            act.activation(xn[:, n, :], xa[:, (ring + 1) % RING, n, :], ACT.Identity,
                                           bias=ln1[:, 3, n:n + 1], scale=ln1[:, 2, n:n + 1]).then_inc(xn_done, 1)
                    if slot == 8 and on(it, has_next):
                        wait(act, aux_filled, aux_use(it, "Qtr") + 1)
                        act.copy(xnT[:, :], aux_ps[:, :]).then_inc(aux_free, 1)
                    if slot == 9 and isinstance(it, int) and it == 0:
                        act.wait_ge(pe_set, 3)
                        act.copy(wt_T[:, :], pv_ps[:, 0:64].bitcast(BF16)).then_inc(act_set, 1)
                    if slot == 10 and c:
                        wait(act, aux_filled, aux_use(it, "Ctr") + 1)
                        act.copy(xqT[:, :], aux_ps[:, 0:256].bitcast(BF16)).then_inc(aux_free, 1)

            run_turns(act, turn)

        @block.vector
        def _(dve):
            for n in range(RING):
                dve.memset(v_ones[n][:, :, :, :], 0.0).then_inc(dve_set, 1)
            dve.wait_ge(dve_set, RING)
            for n in range(RING):
                for e in range(2):
                    dve.memset(v_ones[n][:, :, e, 16 * e + D:16 * e + 2 * D], 1.0).then_inc(dve_set, 1)
            dve.wait_ge(dve_set, 3 * RING)

            def stats(src, st, tiles, signal):
                for n in tiles:
                    dve.bn_stats(st[:, n, :], src[:, n, :]).then_inc(signal, 1)

            def moments(st, mv, b, ready, signal):
                wait(dve, ready, (b + 1) * NT)
                apart(dve, b)
                for n in range(NT):
                    dve.bn_aggr(mv[:, n, :], st[:, n, :]).then_inc(signal, 1)

            def maxima(b, place):
                for k in PLACES[place]:
                    g, tiles = STEPS[k]
                    wait(dve, max_ready, b * NSTEP + (k + 1))
                    if k == 0:
                        wait(dve, m_split, b * 5)
                    n = len(tiles)
                    width = GRP * (g + 1)
                    src = max_ps[:, k % 3, 0:n * width].rearrange("p (n w) -> p n w", n=n)
                    dve.tensor_reduce(neg_max[:, tiles[0]:tiles[0] + n], src, AX_X, ALU.max,
                                      negate=True).then_inc(max_done, 1)

            def invert(it, b, pair, name):
                wait(dve, aux_filled, aux_use(it, name) + 1)
                bank = aux_ps[:, :].rearrange("p (nj k) -> p nj k", k=2 * D)
                dve.reciprocal(y_inv[:, :], bank[:, :, D]).then_inc(inv_done, 1)

            def normalise(b, pair):
                wait(dve, inv_done, b * 2 + (pair + 1))
                bank = aux_ps[:, :].rearrange("p (nj k) -> p nj k", k=2 * D)
                inv = y_inv[:, :].rearrange("p (a b) -> p a b", b=1).broadcast_to([128, NT * H // 2, D])
                half = y_t[:, :, 64 * pair:64 * pair + 64].rearrange("p n (j d) -> p n j d", d=D)
                dve.tensor_tensor(half, bank[:, :, 0:D], inv, ALU.mult).then_inc(aux_free, 1)

            def turn(it, ring):
                q, m, b, c = (on(it, s) for s in (has_q, has_m, has_b, has_c))
                for at in [(slot, place) for slot in range(SLOTS) for place in range(4)]:
                    if at == (0, 0) and b:
                        wait(dve, max_done, (it - 1) * NSTEP)
                        if not isinstance(it, int) or it > 2:
                            wait(dve, aux_filled, aux_use(it - 1, "Msel") + 1)
                        dve.tensor_copy(m_parts[:, 0, :], neg_max[:, :]).then_inc(m_split, 1)
                        wait(dve, m_split, it * 5 - 9)
                        dve.tensor_tensor(m_r[:, 0, :], neg_max[:, :], m_parts[:, 0, :], ALU.subtract).then_inc(m_split, 1)
                        wait(dve, m_split, it * 5 - 8)
                        dve.tensor_copy(m_parts[:, 1, :], m_r[:, 0, :]).then_inc(m_split, 1)
                        wait(dve, m_split, it * 5 - 7)
                        dve.tensor_tensor(m_r[:, 1, :], m_r[:, 0, :], m_parts[:, 1, :], ALU.subtract).then_inc(m_split, 1)
                        wait(dve, m_split, it * 5 - 6)
                        dve.tensor_copy(m_parts[:, 2, :], m_r[:, 1, :]).then_inc(m_split, 1)
                    if m:
                        maxima(it - 1, 4 * at[0] + at[1])
                    if at == (1, 3) and q:
                        wait(dve, k1_done, it + 1)
                        wait(dve, kf_done, it)
                        dve.tensor_tensor(k_r[:, :], aux_ps[0:KV, :], k1[:, :], ALU.subtract).then_inc(aux_free, 1)
                    if at == (2, 3) and q:
                        wait(dve, q1_done, it + 1)
                        wait(dve, q3_done, it)
                        dve.tensor_tensor(positions(q_r), by_position(aux_ps), positions(q1),
                                          ALU.subtract).then_inc(aux_free, 1)
                    if at == (2, 0) and on(it, has_next):
                        wait(dve, x_loaded, (it + 2) * 16)
                        apart(dve, it)
                        wait(dve, ln1_step, (it + 1) * 4)
                        stats(xa[:, (ring + 1) % RING], st1, range(0, 2), ln1_stats)
                    if at == (2, 1) and on(it, has_next):
                        stats(xa[:, (ring + 1) % RING], st1, range(2, NT), ln1_stats)
                    if at == (3, 0) and on(it, has_next):
                        moments(st1, mv1, it + 1, ln1_stats, ln1_aggr)
                    if isinstance(it, int) and it == FIRST_TURN and at == (4, 0):
                        dve.wait_ge(w_loaded, 16 * N_WEIGHTS)
                        dve.tensor_scalar(scale_sb[:, 1:2], scale_sb[:, 0:1], EPS, None, ALU.max).then_inc(dve_set, 1)
                        dve.wait_ge(dve_set, 3 * RING + 1)
                        dve.reciprocal(scale_sb[:, 2:3], scale_sb[:, 1:2]).then_inc(dve_set, 1)
                        dve.tensor_scalar(wt_b[:, :], wt_i[:, :], -1.0, None, ALU.add).then_inc(dve_set, 1)
                        dve.tensor_scalar(scale_sb[:, 3:4], scale_sb[:, 1:2], BIGGEST, 0.5, ALU.min, ALU.mult).then_inc(dve_set, 1)
                        dve.wait_ge(dve_set, 3 * RING + 4)
                    for pair, name in enumerate(("Ya", "Yb")):
                        if at == (3 + pair, 2) and c:
                            invert(it, it - 3, pair, name)
                        if at == (3 + pair, 3) and c:
                            normalise(it - 3, pair)
                    if at == (6, 2) and c:
                        wait(dve, aux_filled, aux_use(it, "Cproj") + 1)
                        wait(dve, xr_loaded, (it - 2) * 32)
                        dve.tensor_tensor(x1[:, :, :], aux_ps[:, :].rearrange("p (n c) -> p n c", n=NT), xr[:, :, :],
                                          ALU.add).then_inc(aux_free, 1)
                    if at == (6, 3) and c:
                        wait(dve, aux_free, aux_use(it, "Cproj") + 1)
                        apart(dve, it)
                        stats(x1, st2, range(0, 2), ln2_stats)
                    if at == (7, 0) and c:
                        stats(x1, st2, range(2, NT), ln2_stats)
                    if at == (7, 1) and c:
                        moments(st2, mv2, it - 3, ln2_stats, ln2_aggr)
                    if at == (7, 2) and q:
                        wait(dve, aux_filled, aux_use(it, "Qv") + 1)
                        wait(dve, pv_done, (it - 2) * UNITS)
                        v = v_ones[ring][:, :, :, :].rearrange("p n e x -> p n (e x)")
                        for e in range(2):
                            s = dve.tensor_copy(v[:, :, 48 * e:48 * e + D],
                                                aux_ps[:, 0:NT * 16].rearrange("p (n d) -> p n d", n=NT)[:, :, KQ - 64:KV - 64])
                        s.then_inc(aux_free, 1)
                    if at == (9, 3) and c:
                        wait(dve, zb_done, it - 2)
                        dve.tensor_scalar(z_lo[:, :, :], zb[:, :, :], QB, -QB, ALU.min, ALU.max).then_inc(clipped, 1)
                        dve.tensor_scalar(z_hi[:, :, :], zb[:, :, :], -QB, QB, ALU.max, ALU.min).then_inc(clipped, 1)
                    if at == (10, 0) and c:
                        wait(dve, clipped, (it - 2) * 2)
                        dve.tensor_tensor(xq[:, :, :], z_lo[:, :, :], z_hi[:, :, :], ALU.add).then_inc(xq_done, 1)
                    if at == (11, 3) and c:
                        wait(dve, aux_filled, aux_use(it, "Cffn") + 1)
                        wait(dve, x1b_done, it - 2)
                        wait(dve, o_stored, (it - 2) * 32)
                        dve.scalar_tensor_tensor(out=o_sb[:, :, :].rearrange("p n c -> p (n c)"), in0=aux_ps[:, :],
                                                 scalar=scale_sb[:, 3:4],
                                                 in1=x1b[:, :, :].rearrange("p n c -> p (n c)"),
                                                 op0=ALU.mult, op1=ALU.add).then_inc(aux_free, 1)

            run_turns(dve, turn)

        @block.gpsimd
        def _(pool):
            count = [0]

            def done(ins):
                ins.then_inc(pool_set, 1)
                count[0] += 1
                pool.wait_ge(pool_set, count[0])

            def keep(tile, compare, fill, base, pattern, channel):
                done(pool.affine_select(out=tile, in_=tile, compare_op=compare, fill=fill, base=base,
                                        pattern=pattern, channel_multiplier=channel))

            for square in (ident, ident_b):
                done(pool.memset(square[:, :], 0.0))
                keep(square[:, :], ALU.not_equal, 1.0, 0, [[-1, 128]], 1)
            done(pool.memset(half_neg[:, :], -0.5))
            done(pool.memset(part_row[:, :, :, :], 0.0))
            for n in range(2):
                by_part = part_row[:, n, 0:PARTS * PARTS].rearrange("o (a b) d -> o a b d", b=PARTS)
                done(pool.memset(by_part[:, :, n + 1:PARTS], 1.0))
            assert count[0] == PART_SET
            done(pool.memset(one_hot[:, :, :], 0.0))
            hot = one_hot[64:96].rearrange("p a (g b) -> p a g b", b=GRP // TQ)
            keep(hot, ALU.not_equal, 1.0, R_MASK - 64, [[1, TQ], [0, T // GRP], [TQ, GRP // TQ]], -1)
            assert count[0] == HOT_SET

            def set_up_rows():
                for n in range(RING):
                    done(pool.memset(k_rows[n][64:96, :], 0.0))
                    done(pool.memset(k_rows[n][96:128, :], 1.0))
                    done(pool.memset(k_mask[n][64:96, :], 0.0))
                    keep(k_mask[n][64:96, :].rearrange("p (g t) -> p g t", t=GRP), ALU.is_ge, NEG, -(R_MASK - 64),
                         [[0, T // GRP], [-1, GRP]], 1)
                done(pool.memset(select[:, :, :], 0.0))
                keep(select[:, :, :], ALU.not_equal, 1.0, TQ * 32, [[-1, TQ], [-TQ, 80]], 1)
                assert count[0] == POOL_SET

            def small_ln(mv, ln, step, b, per, aggr):
                wait(pool, aggr, (b + 1) * NT)
                apart(pool, b)
                pool.tensor_scalar(ln[:, 0, :], mv[:, :, 1], EPS, 1.0, ALU.add, ALU.mult).then_inc(step, 1)
                pool.tensor_scalar(ln[:, 1, :], mv[:, :, 0], -1.0, 0.0, ALU.mult, ALU.add).then_inc(step, 1)
                wait(pool, step, b * per + 2)
                pool.tensor_tensor(ln[:, 2, :], ln[:, 0, :], half_neg[:, :], ALU.pow).then_inc(step, 1)
                wait(pool, step, b * per + 3)

            def small_ln1(b):
                wait(pool, xn_done, b * NT)
                small_ln(mv1, ln1, ln1_step, b, 4, ln1_aggr)
                pool.tensor_tensor(ln1[:, 3, :], ln1[:, 1, :], ln1[:, 2, :], ALU.mult).then_inc(ln1_step, 1)

            def select_causal(b, unit):
                hq, kind = divmod(unit, 3)
                wait(pool, exp_done, b * CHUNKS + (10 * hq + (4, 8, 10)[kind]))
                apart(pool, b)
                tiles = probs[kind][:, :].rearrange("p (ra i) -> p ra i", i=32 if kind == 2 else 64)
                for at in {0: [0], 1: [0, 48], 2: [0]}[kind]:
                    v = tiles[:, :, at:at + 16]
                    pool.affine_select(out=v, in_=v, compare_op=ALU.is_ge, fill=0.0, base=0,
                                       pattern=[[0, 4], [1, TQ], [TQ, 16]],
                                       channel_multiplier=-1).then_inc(masked, 1)

            def normalise2(b):
                small_ln(mv2, ln2, ln2_step, b, 5, ln2_aggr)
                apart(pool, b)
                pool.tensor_scalar(ln2[:, 4, :], ln2[:, 2, :], scale_sb[:, 2:3], 0.0, ALU.mult, ALU.add).then_inc(ln2_step, 1)
                wait(pool, ln2_step, b * 5 + 4)
                pool.tensor_tensor(ln2[:, 3, :], ln2[:, 1, :], ln2[:, 4, :], ALU.mult).then_inc(ln2_step, 1)
                wait(pool, ln2_step, (b + 1) * 5)
                apart(pool, b)

            def scale_x1(tiles):
                for n in tiles:
                    pool.tensor_scalar(z[:, n, :], x1[:, n, :], ln2[:, 4, n:n + 1], ln2[:, 3, n:n + 1],
                                       ALU.mult, ALU.add).then_inc(z_step, 1)

            def round_z(b):
                wait(pool, z_step, b * (NT + 1) + NT)
                apart(pool, b)
                pool.tensor_scalar(z_up[:, :, :], z[:, :, :], 1.0, ROUND, ALU.mult, ALU.add).then_inc(z_step, 1)
                wait(pool, z_step, (b + 1) * (NT + 1))
                apart(pool, b)
                pool.tensor_scalar(zb[:, :, :], z_up[:, :, :], -ROUND, 1.0, ALU.add, ALU.mult).then_inc(zb_done, 1)


            def turn(it, ring):
                q, m, b, c = (on(it, s) for s in (has_q, has_m, has_b, has_c))
                for slot in range(SLOTS):
                    if slot < B_LATE and c:
                        select_causal(it - 3, UNITS - B_LATE + slot)
                    if slot >= B_LATE and b:
                        select_causal(it - 2, slot - B_LATE)
                    if slot == 2 and q:
                        wait(pool, aux_free, aux_use(it, "Qk") + 1)
                        wait(pool, k_moved, it * 32)
                        apart(pool, it)
                        pool.tensor_scalar(k2[:, :], k_r[0:KQ, :], part_col[0:KQ, 1:2], 0.0, ALU.mult, ALU.add).then_inc(k2_done, 1)
                        wait(pool, k2_done, it + 1)
                        pool.tensor_tensor(kf[:, :], k_r[0:KQ, :], k2[:, :], ALU.subtract).then_inc(kf_done, 1)
                    if slot == 3 and q:
                        wait(pool, aux_free, aux_use(it, "Qq") + 1)
                        wait(pool, q_moved, it * 16 * PARTS * PARTS)
                        apart(pool, it)
                        pool.tensor_scalar(q2[:, :], q_r[:, :], 1.0, 0.0, ALU.mult, ALU.add).then_inc(q2_done, 1)
                        wait(pool, q2_done, it + 1)
                        pool.tensor_tensor(q3[:, :], q_r[:, :], q2[:, :], ALU.subtract).then_inc(q3_done, 1)
                    if slot == 4 and on(it, has_next):
                        small_ln1(it + 1)
                    if isinstance(it, int) and it == FIRST_TURN and slot == 4:
                        pool.wait_ge(ln1_step, 4)
                        set_up_rows()
                        pool.wait_ge(w_loaded, 16 * N_WEIGHTS)
                        pool.wait_ge(dve_set, 3 * RING + 4)
                        pool.wait_ge(part_moved, 32)
                    if slot == 7 and c:
                        normalise2(it - 3)
                        scale_x1(range(0, 2))
                    if slot == 8 and c:
                        scale_x1(range(2, NT))
                        if not isinstance(it, int) or it > 3:
                            wait(pool, aux_free, aux_use(it - 1, "Cffn") + 1)
                        round_z(it - 3)
                    if slot == 9 and c:
                        pool.tensor_tensor(x1b[:, :, :], x1[:, :, :],
                                           bias_sb[:, :].rearrange("p (a c) -> p a c", a=1).broadcast_to([128, NT, C]),
                                           ALU.add).then_inc(x1b_done, 1)

            run_turns(pool, turn)


_INS = ["L0_attn_x", "L0_attn_Wc_down", "L0_attn_Wq_up", "L0_attn_Wkv_up", "L0_attn_Wc_proj",
        "L0_ffn_ternary_weight", "L0_ffn_bias", "L0_ffn_act_scale"]


def kernel(**inputs):
    import numpy as _np
    import concourse.bacc as _bacc
    from concourse import mybir as _mybir
    from concourse.bass_utils import run_bass_kernel_spmd as _run

    nc = _bacc.Bacc("TRN2", target_bir_lowering=False, num_devices=1)
    arrays, args = {}, []
    for name in _INS:
        a = _np.ascontiguousarray(inputs[name])
        if name == "L0_ffn_act_scale":
            a = a.reshape(1, 1)
        arrays[f"in_{name}_dram"] = a
        args.append(nc.dram_tensor(f"in_{name}_dram", a.shape, _mybir.dt.from_np(a.dtype), kind="ExternalInput").ap())
    args.append(nc.dram_tensor("out_dram", (NB, T, C), _mybir.dt.float32, kind="ExternalOutput").ap())
    program(nc, *args)
    r = _run(nc, [arrays], core_ids=[0])
    return r.results[0]["out_dram"]
```
